# Optimizing a Trainium2 kernel written in Bass

```python
import numpy as np
import jax
import jax.numpy as jnp

def _softmax(x, axis=-1):
    return jax.nn.softmax(x, axis=axis)

def _gelu(x):
    return jax.nn.gelu(x, approximate=True)

def _silu(x):
    return jax.nn.silu(x)

def _sigmoid(x):
    return jax.nn.sigmoid(x)

def _layernorm(x, axis=-1, eps=1e-05):
    m = jnp.mean(x, axis=axis, keepdims=True)
    v = jnp.var(x, axis=axis, keepdims=True)
    return (x - m) / jnp.sqrt(v + eps)

def _scatter_add(tgt, idx, src, axis=0):
    return tgt.at[idx].add(src)

def _segment_sum(src, seg, n):
    return jax.ops.segment_sum(src, seg, n)
kernel_name = 'mk_gnn_resnorm_d1_gnn_r8_2703f1'

def setup_inputs(seed: int=0):
    np.random.seed(seed)
    _w = jnp.asarray

    def _rec_inputs():
        import jax
        import jax.numpy as jnp
        _gk = jax.random.key(seed)
        x = -0.000202 + 1 * jax.random.normal(jax.random.fold_in(_gk, 1), (6250, 128), jnp.float32)
        src = jax.random.randint(jax.random.fold_in(_gk, 2), (100000,), 0, 6250, jnp.int32)
        dst = jax.random.randint(jax.random.fold_in(_gk, 3), (100000,), 0, 6250, jnp.int32)
        _o = jnp.argsort(dst, stable=True)
        src = src[_o]
        dst = dst[_o]
        edge_weight = jax.random.uniform(jax.random.fold_in(_gk, 12), (100000,), jnp.float32, 0.0, 0.999998)
        return (x, src, dst, edge_weight)
    x, src, dst, edge_weight = _rec_inputs()

    def _L0_gnn_setup():
        import jax, jax.numpy as jnp
        import numpy as np
        N, C, E = (6250, 128, 75000)
        EPS = 1e-05
        SLOPE = 0.2

        def layer_norm(h, g, b):
            m = jnp.mean(h, axis=-1, keepdims=True)
            v = jnp.mean((h - m) ** 2, axis=-1, keepdims=True)
            return (h - m) * jax.lax.rsqrt(v + EPS) * g + b
        key = jax.random.key(seed)
        ks = jax.random.split(key, 12)
        s1 = 1.0 / np.sqrt(2 * C)
        s2 = 1.0 / np.sqrt(C)
        return {'x': jax.random.normal(ks[0], (N, C), dtype=jnp.float32), 'edge_index': jax.random.randint(ks[1], (2, E), 0, N, dtype=jnp.int64), 'edge_attr': jax.random.uniform(ks[2], (E,), dtype=jnp.float32), 'w1': jax.random.uniform(ks[3], (2 * C, C), jnp.float32, -s1, s1), 'b1': jax.random.uniform(ks[4], (C,), jnp.float32, -s1, s1), 'g1': jnp.ones((C,), jnp.float32), 'be1': jnp.zeros((C,), jnp.float32), 'w2': jax.random.uniform(ks[5], (C, C), jnp.float32, -s2, s2), 'b2': jax.random.uniform(ks[6], (C,), jnp.float32, -s2, s2), 'g2': jnp.ones((C,), jnp.float32), 'be2': jnp.zeros((C,), jnp.float32)}
    _L0_gnn_all = _L0_gnn_setup()
    _L0_gnn_in = {k: v for k, v in _L0_gnn_all.items() if k in ('w1', 'b1', 'g1', 'be1', 'w2', 'b2', 'g2', 'be2')}
    del _L0_gnn_all
    return {'x': x, 'src': src, 'dst': dst, 'edge_weight': edge_weight, 'L0_gnn_w1': _L0_gnn_in['w1'], 'L0_gnn_b1': _L0_gnn_in['b1'], 'L0_gnn_g1': _L0_gnn_in['g1'], 'L0_gnn_be1': _L0_gnn_in['be1'], 'L0_gnn_w2': _L0_gnn_in['w2'], 'L0_gnn_b2': _L0_gnn_in['b2'], 'L0_gnn_g2': _L0_gnn_in['g2'], 'L0_gnn_be2': _L0_gnn_in['be2']}

def reference(x, src, dst, edge_weight, L0_gnn_w1, L0_gnn_b1, L0_gnn_g1, L0_gnn_be1, L0_gnn_w2, L0_gnn_b2, L0_gnn_g2, L0_gnn_be2):
    import jax
    import jax.numpy as jnp

    def _L0_gnn_ref(x, edge_index, edge_attr, w1, b1, g1, be1, w2, b2, g2, be2):
        import jax, jax.numpy as jnp
        import numpy as np
        N, C, E = (6250, 128, 75000)
        EPS = 1e-05
        SLOPE = 0.2

        def layer_norm(h, g, b):
            m = jnp.mean(h, axis=-1, keepdims=True)
            v = jnp.mean((h - m) ** 2, axis=-1, keepdims=True)
            return (h - m) * jax.lax.rsqrt(v + EPS) * g + b
        source, target = (edge_index[0], edge_index[1])
        ef = jnp.concatenate([x[source], x[target]], axis=1)
        h = jax.nn.leaky_relu(layer_norm(ef @ w1 + b1, g1, be1), SLOPE)
        h = jax.nn.leaky_relu(layer_norm(h @ w2 + b2, g2, be2), SLOPE)
        h = h * edge_attr[:, None]
        out = jax.ops.segment_sum(h, target, num_segments=N)
        return out
    edge_index = jnp.stack([src, dst])
    x = _layernorm(x + _L0_gnn_ref(x, edge_index, edge_weight, L0_gnn_w1, L0_gnn_b1, L0_gnn_g1, L0_gnn_be1, L0_gnn_w2, L0_gnn_b2, L0_gnn_g2, L0_gnn_be2), axis=-1)
    return x

_drawn_inputs = setup_inputs


def setup_inputs(seed=0):
    import zlib

    import numpy as np

    out = dict(_drawn_inputs(seed))
    spreads = {'L0_gnn_g1': (1.0, 0.2),
     'L0_gnn_be1': (0.0, 0.1),
     'L0_gnn_g2': (1.0, 0.2),
     'L0_gnn_be2': (0.0, 0.1)}
    factors = {}
    for name, (base, spread) in spreads.items():
        noise = np.random.default_rng([zlib.crc32(name.encode()), seed]).standard_normal(out[name].shape)
        drawn = base * np.exp(spread * noise) if base else spread * noise
        out[name] = jnp.asarray(drawn.astype(out[name].dtype))
    for name, factor in factors.items():
        out[name] = (out[name] * factor).astype(out[name].dtype)
    return out
```

```python
from contextlib import ExitStack

import concourse.bass as bass
from concourse import mybir

F32 = mybir.dt.float32
BF16 = mybir.dt.bfloat16
I32 = mybir.dt.int32
I16 = mybir.dt.int16
ALU = mybir.AluOpType
ACT = mybir.ActivationFunctionType
AX = mybir.AxisListType

P = 128
C = 128
T = 4
GE = T * P
K = 4
W = 64
HOP = 32
MARGIN = 16
SPAN = HOP * (K - 1) + W
WIDE = 512
EPS = 1e-5
SLOPE = 0.2


def gnn_layer(nc, x, src, dst, ew, w1, b1, g1, be1, w2, b2, g2, be2, out):
    N = x.shape[0]
    E = src.shape[0]
    SE = K * GE
    S = (E + SE - 1) // SE
    G = S * K
    NT = G * T
    IB = 7
    BT = NT // IB
    HB = ((0, 4), (4, IB))
    NN = (N + P - 1) // P
    NL = N - (NN - 1) * P
    NQ = (NN + 3) // 4
    XL = [0, 4, 12, 24, 36, NN]
    ROWS = (MARGIN + N + SPAN + P - 1) // P * P
    NW = (N + WIDE - 1) // WIDE
    FT = E // P
    RE = E - FT * P
    rest_e = E % SE
    own_e = rest_e - (K - 1) * GE
    dst_pieces = 1 if rest_e == 0 else 2 + -(-(SE - rest_e) // own_e)
    assert BT * IB == NT and BT <= P and S <= P and G % 2 == 0
    assert rest_e == 0 or own_e > 0
    assert RE > 0 and (IB - 1) * BT < FT < NT

    ctx = ExitStack()
    with ctx:
        def sb(name, shape, dt):
            return ctx.enter_context(nc.sbuf_tensor(name, shape, dt))

        def psum(name, shape, dt=F32):
            return ctx.enter_context(nc.psum_tensor(name, shape, dt))

        def sem(name):
            return ctx.enter_context(nc.semaphore(name))

        def sems(name, n=K):
            return [sem(f"{name}{k}") for k in range(n)]

        src_table = nc.dram_tensor("src_table", (NN * P, C), F32, kind="Internal").ap()
        dst_table = [nc.dram_tensor(f"dst_table{i}", (ROWS, C), BF16, kind="Internal").ap() for i in range(3)]
        dst16_dram = nc.dram_tensor("dst16_dram", (NT * P,), I16, kind="Internal").ap()

        W1S, W1D, W2, B1, B2 = range(5)
        raw = sb("raw", [P, 5, C], F32)
        mid = sb("mid", [P, 5, C], F32)
        raw_st = sb("raw_st", [P, 5, 6], F32)
        raw_mv = sb("raw_mv", [P, 5, 2], F32)
        b_part = sb("b_part", [P, 2, 3, C], BF16)
        b_rest = sb("b_rest", [P, 2, C], F32)
        b1_rows = sb("b1_rows", [P, 4, C], BF16)
        b2_rows = sb("b2_rows", [P, 4, C], BF16)
        g2_bc = sb("g2_bc", [P, C], F32)
        be2_bc = sb("be2_bc", [P, T, C], F32)
        g1_col = sb("g1_col", [P, 1], F32)
        be1_col = sb("be1_col", [P, 1], F32)
        eps_col = sb("eps_col", [P, 1], F32)
        ones_bf = sb("ones_bf", [P, P], BF16)
        ones_f = sb("ones_f", [P, P], F32)
        ident = sb("ident", [P, P], F32)
        ident_bf = sb("ident_bf", [P, P], BF16)
        iota_row = sb("iota_row", [P, W], F32)
        iota_col = sb("iota_col", [P, 1], F32)
        iota_wide = sb("iota_wide", [P, WIDE], F32)
        wide_off = sb("wide_off", [P, NW], F32)
        win_off = sb("win_off", [P, K], F32)
        zero_bf = sb("zero_bf", [P, C], BF16)

        src_t = sb("src_t", [BT, IB, P], I32)
        dst_t = sb("dst_t", [BT, IB, P], I32)
        ew_t = sb("ew_t", [BT, IB, P], F32)
        src_tf = sb("src_tf", [BT, IB, P], F32)
        dst_tf = sb("dst_tf", [BT, IB, P], F32)
        dst16_t = sb("dst16_t", [BT, IB, P], I16)
        src_idx = sb("src_idx", [P, NT + 2 * T], I32)
        dst_idx = sb("dst_idx", [P, NT + 2 * T], I32)
        dst_f = sb("dst_f", [P, NT], F32)
        ew_all = sb("ew_all", [P, NT], F32)
        dst_rel = sb("dst_rel", [P, S, K, T], F32)
        dst_s = sb("dst_s", [S, K, GE], I32)
        dst_min = sb("dst_min", [S, K], F32)
        dst_max = sb("dst_max", [S, K], F32)
        miss = sb("miss", [S, 2, K], F32)
        base_col = sb("base_col", [S, 1], F32)
        base_diag = sb("base_diag", [S, S + 1], F32)
        base_bc = sb("base_bc", [P, S], F32)
        base_i = sb("base_i", [1, S + 1], I32)
        win_node = sb("win_node", [P, S, K], F32)

        x_all = sb("x_all", [P, NN, C], F32)
        xnT = sb("xnT", [P, 2, 4 * P], F32)
        tab_src = sb("tab_src", [P, 2, 4, C], F32)
        tab_hi = sb("tab_hi", [P, 2, 4, C], BF16)
        tab_mid = sb("tab_mid", [P, 2, 4, C], BF16)
        tab_lo = sb("tab_lo", [P, 2, 4, C], BF16)
        tab_rest = sb("tab_rest", [P, 2, 4, C], F32)
        ACOLS = max(ROWS, MARGIN + NW * WIDE)
        acc = sb("acc", [P, ACOLS], F32)

        idx_slot = sb("idx_slot", [P, K, T], I32)
        a_src = sb("a_src", [P, K, T, C], F32)
        dst_bc = sb("dst_bc", [P, K, GE], I16)
        pick = sb("pick", [P, 2, GE], BF16)
        win_hm = sb("win_hm", [P, K, C], BF16)
        win_lo = sb("win_lo", [W, K, C], BF16)
        junk = sb("junk", [P, 2, 2, T, C], BF16)
        ssq1 = sb("ssq1", [P, 2, T], F32)
        ssq2 = sb("ssq2", [P, 2, T], F32)
        std1 = sb("std1", [P, 2, T], F32)
        std2 = sb("std2", [P, 2, T], F32)
        rstd1 = sb("rstd1", [P, 2, T], F32)
        rstd2 = sb("rstd2", [P, 2, T], F32)
        cn = sb("cn", [P, 2, T, C], F32)
        aff = sb("aff", [P, 2, GE], F32)
        z = sb("z", [P, 2, GE], F32)
        t2 = sb("t2", [P, T, C], F32)
        u2 = sb("u2", [P, T, C], F32)
        y = sb("y", [P, K, T, C], F32)
        seg = sb("seg", [P, K, T, W], F32)

        idx2_slot = sb("idx2_slot", [P, 2, T], I32)
        b_dst = sb("b_dst", [P, 3, T, C], BF16)
        seg_wide = sb("seg_wide", [P, T, WIDE], F32)

        res = sb("res", [P, 2, 4, C], F32)
        stf = sb("stf", [P, 2, 4, 6], F32)
        mvf = sb("mvf", [P, 2, 4, 2], F32)
        stdf = sb("stdf", [P, 2, 4], F32)
        rstdf = sb("rstdf", [P, 2, 4], F32)
        nbias = sb("nbias", [P, 2, 4], F32)
        fin = sb("fin", [P, 2, 4, C], F32)

        ps_c = [psum(f"ps_c{b}", [P, T, C]) for b in range(2)]
        ps_cT = psum("ps_cT", [P, GE])
        ps_h = [psum(f"ps_h{b}", [P, T, C]) for b in range(2)]
        ps_o = psum("ps_o", [P, 512])
        ps_t = [psum(f"ps_t{b}", [P, 512]) for b in range(2)]

        w_in = sem("w_in")
        v_in = sem("v_in")
        src_in = sem("src_in")
        dst_in = sem("dst_in")
        ew_in = sem("ew_in")
        dsts_in = sem("dsts_in")
        x_in = sems("x_in", len(XL) - 1)
        x_tail_in = sem("x_tail_in")
        pads_zero = sem("pads_zero")
        ident_ok = sem("ident_ok")
        iota_ok = sem("iota_ok")
        const_ok = sem("const_ok")
        acc_zero = sem("acc_zero")
        ones_ok = sem("ones_ok")
        dve_own = sem("dve_own")
        centred = sem("centred")
        b_split = sem("b_split")
        src_cast = sem("src_cast")
        dst_cast = sem("dst_cast")
        dst16_cast = sem("dst16_cast")
        turned = sem("turned")
        turn_out = sem("turn_out")
        base_set = sem("base_set")
        base_ps = sem("base_ps")
        base_ok = sem("base_ok")
        rel_ok = sem("rel_ok")
        dst16_out = sem("dst16_out")
        zero_out = sem("zero_out")
        node_T = sem("node_T")
        node_Tc = sem("node_Tc")
        node_A = sem("node_A")
        node_Ac = sem("node_Ac")
        node_B = sem("node_B")
        node_hi = sem("node_hi")
        node_r1 = sem("node_r1")
        node_mid = sem("node_mid")
        node_lo = sem("node_lo")
        src_out = sems("src_out", 2)
        tab_out = sems("tab_out", 2)

        idx_ready = sems("idx_ready")
        gathered = sems("gathered")
        dstbc_in = sems("dstbc_in", 2)
        win_in = sems("win_in", 2)
        pick_ready = sems("pick_ready")
        c_ready = sems("c_ready")
        ssq1_ready = sems("ssq1_ready")
        std1_ready = sems("std1_ready")
        rstd1_ready = sems("rstd1_ready")
        cn_ready = sems("cn_ready")
        cT_ready = sems("cT_ready")
        aff_ready = sems("aff_ready")
        z_ready = sems("z_ready")
        h_ready = sems("h_ready")
        ssq2_ready = sems("ssq2_ready")
        std2_ready = sems("std2_ready")
        rstd2_ready = sems("rstd2_ready")
        t2_ready = sems("t2_ready")
        u2_ready = sems("u2_ready")
        y_ready = sems("y_ready")
        o_ready = sem("o_ready")
        acc_done = sem("acc_done")

        gen_idx = sems("gen_idx", 2)
        gen_gathered = sems("gen_gathered", 2)
        gen = {name: sem("gen_" + name) for name in (
            "c", "ssq1", "std1", "rstd1", "cn", "cT", "aff", "z", "h", "ssq2", "std2", "rstd2", "t2", "u2",
            "y", "seg", "o", "acc")}

        sums_done = sem("sums_done")
        fT_ready = sem("fT_ready")
        res_ready = sem("res_ready")
        stf_ready = sem("stf_ready")
        mvf_ready = sem("mvf_ready")
        stdf_ready = sem("stdf_ready")
        rstdf_ready = sem("rstdf_ready")
        nbias_ready = sem("nbias_ready")
        fin_ready = sem("fin_ready")
        out_done = sems("out_done", 2)

        block = ctx.enter_context(nc.Block())

        def live(s, k, lag):
            if isinstance(s, int):
                return 0 <= K * s + k - lag < G
            return True

        class Back:

            def __init__(self, counts, k, lag):
                self.slot = (k - lag) % K
                self.buf = self.slot % 2
                self.count = counts[(k - lag) // K]

        HEAD = 2

        def supersteps(eng, step):
            for s in range(HEAD):
                step(s, {0: s + 1, -1: s, -2: s - 1})
            with eng.Fori(HEAD, S) as s:
                step(s, {0: eng.snap(s + 1), -1: s, -2: eng.snap(s - 1)})
            for s in range(S, S + HEAD):
                step(s, {0: s + 1, -1: s, -2: s - 1})

        def batch(n):
            return min(4, NN - 4 * n)

        def both_paths(eng, fast, general):
            eng.wait_ge(base_ok, 1)
            misses = eng.value_load(base_i[0:1, S:S + 1], min_val=0, max_val=2 * G)
            with eng.If(misses == 0):
                fast()
            with eng.Else():
                general()

        def act_sum_squares(which, b, bank, ssq):
            for t in range(T):
                ins = nc.scalar.activation(junk[:, which, b, t, :], bank[:, t, :], ACT.Square,
                                           accum_out=ssq[:, b, t:t + 1])
            return ins

        def act_std(ssq, std, b):
            return nc.scalar.activation(std[:, b, :], ssq[:, b, :], ACT.Sqrt, bias=eps_col[:, 0:1], scale=1.0 / C)

        def act_normalise(b, bank):
            for t in range(T):
                ins = nc.scalar.activation(cn[:, b, t, :], bank[:, t, :], ACT.Copy, scale=rstd1[:, b, t:t + 1])
            return ins

        def act_affine(b):
            return nc.scalar.activation(aff[:, b, :], ps_cT[:], ACT.Identity, bias=be1_col[:, 0:1],
                                        scale=g1_col[:, 0:1])

        def pe_source_rows(bank, slot):
            nc.tensor.matmul(bank[:], ident[:], a_src[:, slot, :, :], start=True, stop=True)

        def pe_turn(b):
            for t in range(T):
                mm = nc.tensor.transpose(ps_cT[:, t * P:(t + 1) * P], cn[:, b, t, :], ident[:])
            return mm

        def pe_second_product(b, bank):
            nc.tensor.matmul(bank[:], ones_bf[:], b2_rows[:], start=True, stop=True)
            for t in range(T):
                mm = nc.tensor.matmul(bank[:, t, :], z[:, b, t * P:(t + 1) * P], mid[:, W2, :],
                                      start=False, stop=True, skip_group_check=True)
            return mm

        def dve_leaky1(b):
            return nc.vector.scalar_tensor_tensor(z[:, b, :], aff[:, b, :], SLOPE, aff[:, b, :],
                                                  op0=ALU.mult, op1=ALU.max)

        def dve_scale2(b, bank):
            for t in range(T):
                ins = nc.vector.scalar_tensor_tensor(t2[:, t, :], bank[:, t, :], rstd2[:, b, t:t + 1], g2_bc[:],
                                                     op0=ALU.mult, op1=ALU.mult)
            return ins

        def dve_shift2():
            return nc.vector.tensor_tensor(u2[:], t2[:], be2_bc[:], ALU.add)

        def dve_leaky2(slot):
            return nc.vector.scalar_tensor_tensor(y[:, slot, :, :], u2[:], SLOPE, u2[:], op0=ALU.mult, op1=ALU.max)

        def outs(n, q):
            total = 0
            for i in range(q, n, 2):
                m = batch(i)
                full = m if 4 * i + m < NN or NL == P else m - 1
                total += (full > 0) + (full < m)
            return total

        def store_targets(sp, n):
            m = batch(n)
            sp.wait_ge(node_lo, n + 1)
            r0 = MARGIN + 4 * n * P
            for part, tab in enumerate((tab_hi, tab_mid, tab_lo)):
                sp.dma_start(dst_table[part][r0:r0 + m * P].rearrange("(t p) c -> p t c", p=P),
                             tab[:, n % 2, 0:m, :]).then_inc(tab_out[n % 2], 16)

        @block.sync
        def _(sp):
            sp.dma_start(raw[:, W1S:W1D + 1, :], w1.rearrange("(h p) c -> p h c", p=P)).then_inc(w_in, 16)
            sp.dma_start(raw[:, W2, :], w2).then_inc(w_in, 16)
            sp.dma_start(raw[:, B1, :], b1.partition_broadcast(P)).then_inc(w_in, 16)
            sp.dma_start(raw[:, B2, :], b2.partition_broadcast(P)).then_inc(w_in, 16)
            for i, (a, b) in enumerate(zip(XL[:-1], XL[1:])):
                b = min(b, NN - 1)
                sp.dma_start(x_all[:, a:b, :], x[a * P:b * P].rearrange("(n p) c -> p n c", p=P)).then_inc(x_in[i], 16)
            sp.wait_ge(ones_ok, 1)
            sp.dma_start(x_all[0:NL, NN - 1, :], x[(NN - 1) * P:N]).then_inc(x_tail_in, 16)
            sp.dma_start(g2_bc[:], g2.partition_broadcast(P)).then_inc(v_in, 16)
            for t in range(T):
                sp.dma_start(be2_bc[:, t, :], be2.partition_broadcast(P)).then_inc(v_in, 16)
            sp.dma_start(g1_col[:], g1.rearrange("(p o) -> p o", o=1)).then_inc(v_in, 16)
            sp.dma_start(be1_col[:], be1.rearrange("(p o) -> p o", o=1)).then_inc(v_in, 16)
            zeros = 0
            for r0, r1 in ((0, MARGIN), (MARGIN + NN * P, ROWS)):
                while r0 < r1:
                    n = min(P, r1 - r0)
                    for part in range(3):
                        sp.dma_start(dst_table[part][r0:r0 + n], zero_bf[0:n]).then_inc(zero_out, 16)
                        zeros += 1
                    r0 += n
            for n in range(NQ):
                m = batch(n)
                sp.wait_ge(node_Ac, n + 1)
                sp.dma_start(src_table[4 * n * P:(4 * n + m) * P].rearrange("(t p) c -> p t c", p=P),
                             tab_src[:, n % 2, 0:m, :]).then_inc(src_out[n % 2], 16)
                if n >= 1:
                    store_targets(sp, n - 1)
            store_targets(sp, NQ - 1)
            sp.wait_ge(dst16_cast, 1)
            sp.dma_start(dst16_dram.rearrange("(b p e) -> p b e", b=IB, e=P), dst16_t[:]).then_inc(dst16_out, 16)
            sp.wait_ge(zero_out, 16 * zeros)
            sp.wait_ge(tab_out[0], 48 * ((NQ + 1) // 2))
            sp.wait_ge(tab_out[1], 48 * (NQ // 2))
            sp.wait_ge(dst16_out, 16)

            def step(s, counts):
                first = isinstance(s, int)
                if first and s >= S:
                    return
                base = sp.value_load(base_i[0:1, bass.ds(s, 1)], min_val=0, max_val=N - 1)
                for h in range(2):
                    k0 = 2 * h
                    if not first or s > 0:
                        sp.wait_ge(pick_ready[k0 + 1], counts[-1])
                    at = s * SE + k0 * GE
                    sp.dma_start(dst_bc[:, k0:k0 + 2, :].rearrange("p k e -> p (k e)"),
                                 dst16_dram[bass.ds(at, 2 * GE)].partition_broadcast(P)).then_inc(dstbc_in[h], 16)
                    if not first or s > 0:
                        sp.wait_ge(c_ready[k0 + 1], counts[-1])
                    for part, dest in enumerate((win_hm[0:W], win_hm[W:2 * W], win_lo[:])):
                        for j in range(2):
                            sp.dma_start(dest[:, k0 + j, :],
                                         dst_table[part][bass.ds(base + HOP * (k0 + j), W), :]).then_inc(win_in[h], 16)

            def general():
                sp.wait_ge(base_ok, 1)

            both_paths(sp, lambda: supersteps(sp, step), general)

            for n in range(NQ):
                m = batch(n)
                full = m if 4 * n + m < NN or NL == P else m - 1
                sp.wait_ge(fin_ready, n + 1)
                if full:
                    sp.dma_start(out[4 * n * P:(4 * n + full) * P].rearrange("(t p) c -> p t c", p=P),
                                 fin[:, n % 2, 0:full, :]).then_inc(out_done[n % 2], 16)
                if full < m:
                    sp.dma_start(out[(NN - 1) * P:N], fin[0:NL, n % 2, full, :]).then_inc(out_done[n % 2], 16)
            for q in range(2):
                sp.wait_ge(out_done[q], 16 * outs(NQ, q))

        @block.gpsimd
        def _(pool):
            nc.gpsimd.memset(src_t[:, IB - 1, :], 0)
            nc.gpsimd.memset(dst_t[:, IB - 1, :], 0)
            nc.gpsimd.memset(ew_t[:, IB - 1, :], 0.0).then_inc(pads_zero, 1)
            nc.gpsimd.memset(ident[:], 0.0).then_inc(ident_ok, 1)
            pool.wait_ge(ident_ok, 1)
            nc.gpsimd.affine_select(out=ident[:], in_=ident[:], compare_op=ALU.not_equal, fill=1.0, base=0,
                                    pattern=[[-1, P]], channel_multiplier=1).then_inc(ident_ok, 1)
            nc.gpsimd.iota(iota_row[:], [[1, W]], base=0, channel_multiplier=0,
                           allow_small_or_imprecise_dtypes=True)
            nc.gpsimd.iota(iota_wide[:], [[1, WIDE]], base=0, channel_multiplier=0,
                           allow_small_or_imprecise_dtypes=True)
            nc.gpsimd.iota(wide_off[:], [[WIDE, NW]], base=0, channel_multiplier=0,
                           allow_small_or_imprecise_dtypes=True)
            nc.gpsimd.iota(win_off[:], [[HOP, K]], base=-MARGIN, channel_multiplier=0,
                           allow_small_or_imprecise_dtypes=True)
            nc.gpsimd.iota(iota_col[0:W], [[0, 1]], base=0, channel_multiplier=1,
                           allow_small_or_imprecise_dtypes=True).then_inc(iota_ok, 1)
            pool.wait_ge(iota_ok, 1)
            nc.gpsimd.iota(iota_col[W:2 * W], [[0, 1]], base=0, channel_multiplier=1,
                           allow_small_or_imprecise_dtypes=True).then_inc(const_ok, 1)
            pool.wait_ge(const_ok, 1)
            nc.gpsimd.memset(acc[:], 0.0).then_inc(acc_zero, 1)
            pool.wait_ge(turn_out, 2)
            pool.wait_ge(src_out[0], 16 * ((NQ + 1) // 2))
            pool.wait_ge(src_out[1], 16 * (NQ // 2))

            def gather(dest, table, index, done):
                nc.gpsimd.indirect_dma_start(out=dest, out_offset=None, in_=table,
                                             in_offset=bass.IndirectOffsetOnAxis(ap=index, axis=0)).then_inc(done, 16)

            def step(s, counts):
                first = isinstance(s, int)
                if first and s >= S:
                    return
                for k in range(K):
                    pool.wait_ge(idx_ready[k], counts[0])
                    if not first or s > 0:
                        pool.wait_ge(c_ready[k], counts[-1])
                    nk = (k + 1) % K
                    if not first or s > 0 or nk == 0:
                        pool.wait_ge(gathered[nk], (counts[0] if nk == 0 else counts[-1]) * (16 * T))
                    at = s * (K * T) + (k + 1) * T
                    nc.gpsimd.tensor_copy(idx_slot[:, nk, :], src_idx[:, bass.ds(at, T)]).then_inc(idx_ready[nk], 1)
                    for t in range(T):
                        gather(a_src[:, k, t, :], src_table, idx_slot[:, k, t:t + 1], gathered[k])

            def fast():
                nc.gpsimd.tensor_copy(idx_slot[:, 0, :], src_idx[:, 0:T]).then_inc(idx_ready[0], 1)
                supersteps(pool, step)

            def general():
                pool.wait_ge(turn_out, 6)
                for q in range(2):
                    pool.wait_ge(tab_out[q], 48 * ((NQ + 1 - q) // 2))
                nc.gpsimd.tensor_copy(idx_slot[:, 0, :], src_idx[:, 0:T])
                nc.gpsimd.tensor_copy(idx2_slot[:, 0, :], dst_idx[:, 0:T]).then_inc(gen_idx[0], 1)
                with pool.Fori(0, G // 2) as i:
                    n = pool.snap(i + 1)
                    for b in range(2):
                        before = pool.snap(i * (2 * NW) + (b * NW + 1))
                        pool.wait_ge(gen_idx[b], n)
                        pool.wait_ge(gen["acc"], before)
                        at = i * (2 * T) + (b + 1) * T
                        nc.gpsimd.tensor_copy(idx_slot[:, 1 - b, :], src_idx[:, bass.ds(at, T)])
                        nc.gpsimd.tensor_copy(idx2_slot[:, 1 - b, :], dst_idx[:, bass.ds(at, T)]).then_inc(gen_idx[1 - b], 1)
                        for t in range(T):
                            gather(a_src[:, 0, t, :], src_table, idx_slot[:, b, t:t + 1], gen_gathered[b])
                            for part in range(3):
                                gather(b_dst[:, part, t, :], dst_table[part], idx2_slot[:, b, t:t + 1], gen_gathered[b])

            both_paths(pool, fast, general)

        @block.scalar
        def _(act):
            def tiles_in(dest, dram, done):
                full = (IB - 1) * BT
                act.dma_start(dest[:, 0:IB - 1, :],
                              dram[0:full * P].rearrange("(b p e) -> p b e", b=IB - 1, e=P)).then_inc(done, 16)
                act.wait_ge(pads_zero, 1)
                act.dma_start(dest[0:FT - full, IB - 1, :],
                              dram[full * P:FT * P].rearrange("(p e) -> p e", e=P)).then_inc(done, 16)
                act.dma_start(dest[FT - full:FT - full + 1, IB - 1, 0:RE],
                              dram[FT * P:E].rearrange("(p e) -> p e", p=1)).then_inc(done, 16)

            full = E // SE
            act.dma_start(dst_s[0:full], dst[0:full * SE].rearrange("(s k e) -> s k e", k=K, e=GE)).then_inc(dsts_in, 16)
            if rest_e:
                row = dst_s[full:full + 1].rearrange("s k e -> s (k e)")
                act.dma_start(row[:, 0:rest_e], dst[full * SE:E].rearrange("(s e) -> s e", s=1)).then_inc(dsts_in, 16)
                at = rest_e
                while at < SE:
                    n = min(own_e, SE - at)
                    act.dma_start(row[:, at:at + n], dst[E - n:E].rearrange("(s e) -> s e", s=1)).then_inc(dsts_in, 16)
                    at += n
            tiles_in(src_t, src, src_in)
            tiles_in(dst_t, dst, dst_in)
            tiles_in(ew_t, ew, ew_in)

            def table(n):
                m = batch(n)
                act.wait_ge(node_T, n + 1)
                if n >= 2:
                    act.wait_ge(node_B, n - 1)
                nc.scalar.copy(xnT[:, n % 2, 0:m * P], ps_t[n % 2][:, 0:m * P]).then_inc(node_Tc, 1)
                act.wait_ge(node_A, n + 1)
                if n >= 2:
                    act.wait_ge(src_out[n % 2], 16 * (n // 2))
                nc.scalar.copy(tab_src[:, n % 2, 0:m, :], ps_h[n % 2][:, 0:m, :]).then_inc(node_Ac, 1)
                act.wait_ge(node_B, n + 1)
                if n >= 2:
                    act.wait_ge(tab_out[n % 2], 48 * (n // 2))
                nc.scalar.copy(tab_hi[:, n % 2, 0:m, :], ps_c[n % 2][:, 0:m, :]).then_inc(node_hi, 1)

            def table_mid(n):
                m = batch(n)
                act.wait_ge(node_r1, n + 1)
                nc.scalar.copy(tab_mid[:, n % 2, 0:m, :], tab_rest[:, n % 2, 0:m, :]).then_inc(node_mid, 1)

            for n in range(NQ):
                table(n)
                if n >= 1:
                    table_mid(n - 1)
                if n == 1:
                    act.wait_ge(src_in, 48)
                    nc.scalar.copy(src_tf[:], src_t[:]).then_inc(src_cast, 1)
                if n == 3:
                    act.wait_ge(dst_in, 48)
                    nc.scalar.copy(dst_tf[:], dst_t[:]).then_inc(dst_cast, 1)
                if n == 5:
                    nc.scalar.copy(dst16_t[:], dst_t[:]).then_inc(dst16_cast, 1)
            table_mid(NQ - 1)
            act.wait_ge(v_in, 16 * 7)

            def step(s, counts):
                for k in range(K):
                    if live(s, k, 2):
                        g = Back(counts, k, 2)
                        act.wait_ge(ssq1_ready[g.slot], g.count)
                        act_std(ssq1, std1, g.buf).then_inc(std1_ready[g.slot], 1)
                    if live(s, k, 5):
                        g5 = Back(counts, k, 5)
                        act.wait_ge(h_ready[g5.slot], g5.count)
                        act_sum_squares(1, g5.buf, ps_h[g5.buf], ssq2).then_inc(ssq2_ready[g5.slot], 1)
                    if live(s, k, 3):
                        g = Back(counts, k, 3)
                        act.wait_ge(cT_ready[g.slot], g.count)
                        act_affine(g.buf).then_inc(aff_ready[g.slot], 1)
                    if live(s, k, 5):
                        act.wait_ge(ssq2_ready[g5.slot], g5.count)
                        act_std(ssq2, std2, g5.buf).then_inc(std2_ready[g5.slot], 1)
                    if live(s, k, 2):
                        g = Back(counts, k, 2)
                        act.wait_ge(rstd1_ready[g.slot], g.count)
                        act_normalise(g.buf, ps_c[g.buf]).then_inc(cn_ready[g.slot], 1)
                    if live(s, k, 1):
                        g = Back(counts, k, 1)
                        act.wait_ge(c_ready[g.slot], g.count)
                        act_sum_squares(0, g.buf, ps_c[g.buf], ssq1).then_inc(ssq1_ready[g.slot], 1)

            def general():
                with act.Fori(0, G) as g:
                    n = act.snap(g + 1)
                    act.wait_ge(gen["c"], n)
                    act_sum_squares(0, 0, ps_c[0], ssq1).then_inc(gen["ssq1"], 1)
                    act.wait_ge(gen["ssq1"], n)
                    act_std(ssq1, std1, 0).then_inc(gen["std1"], 1)
                    act.wait_ge(gen["rstd1"], n)
                    act_normalise(0, ps_c[0]).then_inc(gen["cn"], 1)
                    act.wait_ge(gen["cT"], n)
                    act_affine(0).then_inc(gen["aff"], 1)
                    act.wait_ge(gen["h"], n)
                    act_sum_squares(1, 0, ps_h[0], ssq2).then_inc(gen["ssq2"], 1)
                    act.wait_ge(gen["ssq2"], n)
                    act_std(ssq2, std2, 0).then_inc(gen["std2"], 1)

            both_paths(act, lambda: supersteps(act, step), general)

            for n in range(NQ + 1):
                if n < NQ:
                    m = batch(n)
                    act.wait_ge(mvf_ready, n + 1)
                    nc.scalar.activation(stdf[:, n % 2, 0:m], mvf[:, n % 2, 0:m, 1], ACT.Sqrt,
                                         bias=eps_col[:, 0:1]).then_inc(stdf_ready, 1)
                if n >= 1:
                    o = n - 1
                    q = o % 2
                    m = batch(o)
                    act.wait_ge(nbias_ready, n)
                    if o >= 2:
                        act.wait_ge(out_done[q], 16 * outs(o, q))
                    for j in range(m):
                        ins = nc.scalar.activation(fin[:, q, j, :], res[:, q, j, :], ACT.Identity,
                                                   bias=nbias[:, q, j:j + 1], scale=rstdf[:, q, j:j + 1])
                    ins.then_inc(fin_ready, 1)

        @block.tensor
        def _(pe):
            def turn_indices(q, tile_rows, cast, done):
                pe.wait_ge(cast, done)
                for half, (b0, b1_) in enumerate(HB):
                    if q:
                        pe.wait_ge(turn_out, 2 * (q - 1) + half + 1)
                    bank = (ps_cT, ps_o)[half]
                    for blk in range(b0, b1_):
                        at = (blk - b0) * BT
                        mm = nc.tensor.transpose(bank[:, at:at + BT], tile_rows[:, blk, :], ident[0:BT, 0:BT])
                    mm.then_inc(turned, 1)

            def node_turn(n):
                m = batch(n)
                for i, a in enumerate(XL[:-1]):
                    if 4 * n + m > a:
                        pe.wait_ge(x_in[i], 16)
                if n == NQ - 1:
                    pe.wait_ge(x_tail_in, 16)
                if n >= 2:
                    pe.wait_ge(node_Tc, n - 1)
                for j in range(m):
                    mm = nc.tensor.transpose(ps_t[n % 2][:, j * P:(j + 1) * P], x_all[:, 4 * n + j, :], ident[:])
                mm.then_inc(node_T, 1)

            pe.wait_ge(ident_ok, 2)
            node_turn(0)
            pe.wait_ge(centred, 1)
            for n in range(NQ):
                m = batch(n)
                if n + 1 < NQ:
                    node_turn(n + 1)
                pe.wait_ge(node_Tc, n + 1)
                if n >= 2:
                    pe.wait_ge(node_Ac, n - 1)
                for j in range(m):
                    mm = nc.tensor.matmul(ps_h[n % 2][:, j, :], xnT[:, n % 2, j * P:(j + 1) * P], mid[:, W1S, :],
                                          start=True, stop=True)
                mm.then_inc(node_A, 1)
                if n == 0:
                    pe.wait_ge(b_split, 1)
                if n >= 2:
                    pe.wait_ge(node_r1, n - 1)
                bank = ps_c[n % 2]
                nc.tensor.matmul(bank[:, 0:m, :], ones_bf[:], b1_rows[:, 0:m, :], start=True, stop=True)
                for j in range(m):
                    mm = nc.tensor.matmul(bank[:, j, :], xnT[:, n % 2, j * P:(j + 1) * P], mid[:, W1D, :],
                                          start=False, stop=True, skip_group_check=True)
                mm.then_inc(node_B, 1)
                if n == 2:
                    turn_indices(0, src_tf, src_cast, 1)
                if n == 4:
                    turn_indices(1, dst_tf, dst_cast, 1)
                if n == 6:
                    turn_indices(2, ew_t, ew_in, 48)
                if n == 7:
                    pe.wait_ge(base_set, 1)
                    pe.wait_ge(turn_out, 5)
                    nc.tensor.matmul(ps_cT[:, 0:S + 1], ones_f[0:S, :], base_diag[:], start=True,
                                     stop=True).then_inc(base_ps, 1)
            pe.wait_ge(node_r1, NQ)
            pe.wait_ge(node_Ac, NQ)
            pe.wait_ge(turn_out, 6)
            pe.wait_ge(rel_ok, 1)
            pe.wait_ge(b_split, 2)

            def step(s, counts):
                for k in range(K):
                    if live(s, k, 3):
                        g = Back(counts, k, 3)
                        pe.wait_ge(cn_ready[g.slot], g.count)
                        if live(s, k, 4):
                            g4 = Back(counts, k, 4)
                            pe.wait_ge(aff_ready[g4.slot], g4.count)
                        pe_turn(g.buf).then_inc(cT_ready[g.slot], 1)
                    if live(s, k, 4):
                        g = Back(counts, k, 4)
                        if live(s, k, 6):
                            g6 = Back(counts, k, 6)
                            pe.wait_ge(t2_ready[g6.slot], g6.count)
                        pe.wait_ge(z_ready[g.slot], g.count)
                        pe_second_product(g.buf, ps_h[g.buf]).then_inc(h_ready[g.slot], 1)
                    if live(s, k, 1):
                        g = Back(counts, k, 1)
                        if live(s, k, 3):
                            g3 = Back(counts, k, 3)
                            pe.wait_ge(cn_ready[g3.slot], g3.count)
                        pe.wait_ge(gathered[g.slot], g.count * (16 * T))
                        pe_source_rows(ps_c[g.buf], g.slot)
                        pe.wait_ge(pick_ready[g.slot], g.count)
                        pe.wait_ge(win_in[g.slot // 2], g.count * 96)
                        for t in range(T):
                            edges = slice(t * P, (t + 1) * P)
                            nc.tensor.matmul(ps_c[g.buf][:, t, :], pick[:, g.buf, edges], win_hm[:, g.slot, :],
                                             start=False, stop=True, skip_group_check=True)
                            mm = nc.tensor.matmul(ps_c[g.buf][:, t, :], pick[0:W, g.buf, edges], win_lo[:, g.slot, :],
                                                  start=False, stop=True, skip_group_check=True)
                        mm.then_inc(c_ready[g.slot], 1)
                    if live(s, k, 6):
                        g = Back(counts, k, 6)
                        pe.wait_ge(y_ready[g.slot], g.count)
                        if g.slot == 0:
                            pe.wait_ge(acc_done, g.count)
                        at = HOP * g.slot
                        for t in range(T):
                            mm = nc.tensor.matmul(ps_o[:, at:at + W], y[:, g.slot, t, :], seg[:, g.slot, t, :],
                                                  start=(g.slot == 0 and t == 0), stop=True, skip_group_check=True)
                        if g.slot == K - 1:
                            mm.then_inc(o_ready, 1)

            def general():
                with pe.Fori(0, G // 2) as i:
                    for b in range(2):
                        n = pe.snap(2 * i + (b + 1))
                        pe.wait_ge(gen_gathered[b], (i + 1) * (16 * 4 * T))
                        pe_source_rows(ps_c[0], 0)
                        for part in range(3):
                            mm = nc.tensor.matmul(ps_c[0][:], ident_bf[:], b_dst[:, part, :, :], start=False,
                                                  stop=True, skip_group_check=True)
                        mm.then_inc(gen["c"], 1)
                        pe.wait_ge(gen["cn"], n)
                        pe_turn(0).then_inc(gen["cT"], 1)
                        pe.wait_ge(gen["z"], n)
                        pe_second_product(0, ps_h[0]).then_inc(gen["h"], 1)
                        with pe.Fori(0, NW) as w:
                            pe.wait_ge(gen["seg"], i * (2 * NW) + w + (b * NW + 1))
                            for t in range(T):
                                mm = nc.tensor.matmul(ps_o[:], y[:, 0, t, :], seg_wide[:, t, :],
                                                      start=(t == 0), stop=(t == T - 1))
                            mm.then_inc(gen["o"], 1)

            both_paths(pe, lambda: supersteps(pe, step), general)

            pe.wait_ge(sums_done, 1)
            for n in range(NQ):
                m = batch(n)
                if n >= 2:
                    pe.wait_ge(res_ready, n - 1)
                for j in range(m):
                    at = MARGIN + (4 * n + j) * P
                    mm = nc.tensor.transpose(ps_c[n % 2][:, j, :], acc[:, at:at + P], ident[:])
                mm.then_inc(fT_ready, 1)

        @block.vector
        def _(dve):
            own = [0]

            def then(ins):
                own[0] += 1
                ins.then_inc(dve_own, 1)
                dve.wait_ge(dve_own, own[0])

            nc.vector.memset(ones_f[:], 1.0)
            nc.vector.memset(ones_bf[:], 1.0)
            nc.vector.memset(eps_col[:], EPS)
            nc.vector.memset(b1_rows[:], 0.0)
            nc.vector.memset(b2_rows[:], 0.0)
            nc.vector.memset(zero_bf[:], 0.0)
            nc.vector.memset(src_idx[:, NT:NT + 2 * T], 0)
            nc.vector.memset(dst_idx[:, NT:NT + 2 * T], 0)
            nc.vector.memset(x_all[:, NN - 1, :], 0.0).then_inc(ones_ok, 1)
            dve.wait_ge(ones_ok, 1)

            dve.wait_ge(w_in, 64)
            for i in range(5):
                ins = nc.vector.bn_stats(raw_st[:, i, :], raw[:, i, :])
            then(ins)
            for i in range(5):
                ins = nc.vector.bn_aggr(raw_mv[:, i, :], raw_st[:, i, :])
            then(ins)
            for i in range(5):
                ins = nc.vector.tensor_scalar(mid[:, i, :], raw[:, i, :], raw_mv[:, i, 0:1], None, ALU.subtract)
            ins.then_inc(centred, 1)
            dve.wait_ge(centred, 1)

            for i, (b_bc, rows) in enumerate(((mid[:, B1, :], b1_rows), (mid[:, B2, :], b2_rows))):
                then(nc.vector.tensor_copy(b_part[:, i, 0, :], b_bc))
                then(nc.vector.tensor_tensor(b_rest[:, i, :], b_bc, b_part[:, i, 0, :], ALU.subtract))
                then(nc.vector.tensor_copy(b_part[:, i, 1, :], b_rest[:, i, :]))
                then(nc.vector.tensor_tensor(b_part[:, i, 2, :], b_rest[:, i, :], b_part[:, i, 1, :], ALU.subtract))
                for part in range(3):
                    r = 32 * part
                    ins = nc.vector.tensor_copy(rows[r:r + 1, :, :],
                                                b_part[r:r + 1, i, part, :].unsqueeze(1).to_broadcast([1, 4, C]))
                ins.then_inc(b_split, 1)

            def evacuate(q, half, *dests):
                dve.wait_ge(turned, 2 * q + half + 1)
                b0, b1_ = HB[half]
                for dest, shift in dests:
                    view = dest[:, b0 * BT:b1_ * BT]
                    bank = (ps_cT, ps_o)[half][:, 0:(b1_ - b0) * BT]
                    if shift:
                        ins = nc.vector.tensor_scalar(view, bank, float(shift), None, ALU.add)
                    else:
                        ins = nc.vector.tensor_copy(view, bank)
                ins.then_inc(turn_out, 1)

            def table_rest(n):
                m = batch(n)
                dve.wait_ge(node_hi, n + 1)
                nc.vector.tensor_tensor(tab_rest[:, n % 2, 0:m, :], ps_c[n % 2][:, 0:m, :], tab_hi[:, n % 2, 0:m, :],
                                        ALU.subtract).then_inc(node_r1, 1)

            def table_low(n):
                m = batch(n)
                dve.wait_ge(node_mid, n + 1)
                if n >= 2:
                    dve.wait_ge(tab_out[n % 2], 48 * (n // 2))
                nc.vector.tensor_tensor(tab_lo[:, n % 2, 0:m, :], tab_rest[:, n % 2, 0:m, :],
                                        tab_mid[:, n % 2, 0:m, :], ALU.subtract).then_inc(node_lo, 1)

            def least_targets():
                dve.wait_ge(dsts_in, 16 * dst_pieces)
                nc.vector.tensor_reduce(dst_max[:], dst_s[:], AX.X, ALU.max)
                then(nc.vector.tensor_reduce(dst_min[:], dst_s[:], AX.X, ALU.min))
                then(nc.vector.tensor_reduce(base_col[:], dst_min[:], AX.X, ALU.min))
                dve.wait_ge(ident_ok, 2)
                dve.wait_ge(const_ok, 1)
                nc.vector.tensor_scalar(base_diag[:, 0:S], ident[0:S, 0:S], base_col[:, 0:1], None, ALU.mult)
                for i, lim in enumerate((dst_min, dst_max)):
                    ins = nc.vector.scalar_tensor_tensor(miss[:, i, :], lim[:], base_col[:, 0:1], win_off[0:S, :],
                                                         op0=ALU.subtract, op1=ALU.subtract)
                then(ins)
                nc.vector.tensor_scalar(miss[:, 0, :], miss[:, 0, :], 0.0, None, ALU.is_lt)
                then(nc.vector.tensor_scalar(miss[:, 1, :], miss[:, 1, :], float(W - 1), None, ALU.is_gt))
                nc.vector.tensor_reduce(base_diag[:, S:S + 1], miss[:].rearrange("s i k -> s (i k)"), AX.X,
                                        ALU.add).then_inc(base_set, 1)

            def windows():
                dve.wait_ge(base_ps, 1)
                nc.vector.tensor_copy(base_i[:], ps_cT[0:1, 0:S + 1]).then_inc(base_ok, 1)
                then(nc.vector.tensor_copy(base_bc[:], ps_cT[:, 0:S]))
                then(nc.vector.tensor_tensor(dst_rel[:].rearrange("p s k t -> p s (k t)"),
                                             dst_f[:].rearrange("p (s m) -> p s m", s=S),
                                             base_bc[:].unsqueeze(2).to_broadcast([P, S, K * T]), ALU.subtract))
                for k in range(K):
                    off = float(HOP * k - MARGIN)
                    nc.vector.tensor_scalar(dst_rel[:, :, k, :], dst_rel[:, :, k, :], off, None, ALU.subtract)
                    ins = nc.vector.tensor_scalar(win_node[:, :, k], base_bc[:], iota_col[:, 0:1], off, ALU.add, ALU.add)
                ins.then_inc(rel_ok, 1)

            for n in range(NQ):
                table_rest(n)
                if n >= 1:
                    table_low(n - 1)
                if n == 0:
                    least_targets()
                    nc.vector.tensor_copy(ident_bf[:], ident[:])
                if n == 3:
                    evacuate(0, 0, (src_idx, 0))
                    evacuate(0, 1, (src_idx, 0))
                if n == 5:
                    evacuate(1, 0, (dst_f, 0), (dst_idx, MARGIN))
                    evacuate(1, 1, (dst_f, 0), (dst_idx, MARGIN))
                if n == 7:
                    evacuate(2, 0, (ew_all, 0))
                    evacuate(2, 1, (ew_all, 0))
                if n == 8:
                    windows()
            table_low(NQ - 1)
            dve.wait_ge(v_in, 16 * 7)
            dve.wait_ge(rel_ok, 1)
            dve.wait_ge(acc_zero, 1)
            nc.vector.nop().then_inc(acc_done, 1)

            def step(s, counts):
                for k in range(K):
                    g2_, g3, g5 = (Back(counts, k, lag) for lag in (2, 3, 5))
                    if live(s, k, 2):
                        dve.wait_ge(std1_ready[g2_.slot], g2_.count)
                        nc.vector.reciprocal(rstd1[:, g2_.buf, :], std1[:, g2_.buf, :]).then_inc(rstd1_ready[g2_.slot], 1)
                    if k == 2 and live(s, k, 7):
                        base = dve.value_load(base_i[0:1, bass.ds(s - 2, 1)], min_val=0, max_val=N - 1)
                        dve.wait_ge(o_ready, counts[-2])
                        part = acc[:, bass.ds(base, SPAN)]
                        nc.vector.tensor_tensor(part, part, ps_o[:, 0:SPAN], ALU.add).then_inc(acc_done, 1)
                    if live(s, k, 5):
                        for t in range(T):
                            n = s * (K * T) + (k - 5) * T + t
                            nc.vector.tensor_scalar(seg[:, g5.slot, t, :], iota_row[:],
                                                    dst_rel[:].rearrange("p s k t -> p (s k t)")[:, bass.ds(n, 1)],
                                                    ew_all[:, bass.ds(n, 1)], ALU.is_equal, ALU.mult)
                    if live(s, k, 0):
                        dve.wait_ge(dstbc_in[k // 2], counts[0] * 16)
                        nc.vector.tensor_scalar(pick[:, k % 2, :], dst_bc[:, k, :],
                                                win_node[:].rearrange("p s k -> p (s k)")[:, bass.ds(s * K + k, 1)],
                                                None, ALU.is_equal).then_inc(pick_ready[k], 1)
                    if live(s, k, 3):
                        dve.wait_ge(aff_ready[g3.slot], g3.count)
                        dve_leaky1(g3.buf).then_inc(z_ready[g3.slot], 1)
                    if live(s, k, 5):
                        dve.wait_ge(std2_ready[g5.slot], g5.count)
                        nc.vector.reciprocal(rstd2[:, g5.buf, :], std2[:, g5.buf, :]).then_inc(rstd2_ready[g5.slot], 1)
                        dve.wait_ge(rstd2_ready[g5.slot], g5.count)
                        dve_scale2(g5.buf, ps_h[g5.buf]).then_inc(t2_ready[g5.slot], 1)
                        dve.wait_ge(t2_ready[g5.slot], g5.count)
                        dve_shift2().then_inc(u2_ready[g5.slot], 1)
                        dve.wait_ge(u2_ready[g5.slot], g5.count)
                        dve_leaky2(g5.slot).then_inc(y_ready[g5.slot], 1)

            def fast():
                supersteps(dve, step)
                dve.wait_ge(acc_done, S + 1)
                nc.vector.nop().then_inc(sums_done, 1)

            def general():
                nc.vector.nop().then_inc(gen["acc"], 1)
                with dve.Fori(0, G) as g:
                    n = dve.snap(g + 1)
                    dve.wait_ge(gen["std1"], n)
                    nc.vector.reciprocal(rstd1[:, 0, :], std1[:, 0, :]).then_inc(gen["rstd1"], 1)
                    dve.wait_ge(gen["aff"], n)
                    dve_leaky1(0).then_inc(gen["z"], 1)
                    dve.wait_ge(gen["std2"], n)
                    nc.vector.reciprocal(rstd2[:, 0, :], std2[:, 0, :]).then_inc(gen["rstd2"], 1)
                    dve.wait_ge(gen["rstd2"], n)
                    dve_scale2(0, ps_h[0]).then_inc(gen["t2"], 1)
                    dve.wait_ge(gen["t2"], n)
                    dve_shift2().then_inc(gen["u2"], 1)
                    dve.wait_ge(gen["u2"], n)
                    dve_leaky2(0).then_inc(gen["y"], 1)
                    dve.wait_ge(gen["y"], n)
                    for t in range(T):
                        weighted = y[:, 0, t, :]
                        ins = nc.vector.tensor_scalar(weighted, weighted, ew_all[:, bass.ds(g * T + t, 1)], None, ALU.mult)
                    with dve.Fori(0, NW) as w:
                        m = dve.snap(g * NW + w + 1)
                        for t in range(T):
                            ins = nc.vector.tensor_scalar(seg_wide[:, t, :], iota_wide[:], wide_off[:, bass.ds(w, 1)],
                                                          dst_f[:, bass.ds(g * T + t, 1)], ALU.add, ALU.is_equal)
                        ins.then_inc(gen["seg"], 1)
                        dve.wait_ge(gen["o"], m)
                        part = acc[:, bass.ds(w * WIDE + MARGIN, WIDE)]
                        nc.vector.tensor_tensor(part, part, ps_o[:], ALU.add).then_inc(gen["acc"], 1)
                        dve.wait_ge(gen["acc"], dve.snap(m + 1))
                nc.vector.nop().then_inc(sums_done, 1)

            both_paths(dve, fast, general)

            for n in range(NQ + 1):
                if n < NQ:
                    m = batch(n)
                    q = n % 2
                    dve.wait_ge(fT_ready, n + 1)
                    if n >= 2:
                        dve.wait_ge(fin_ready, n - 1)
                    nc.vector.tensor_tensor(res[:, q, 0:m, :], ps_c[q][:, 0:m, :], x_all[:, 4 * n:4 * n + m, :],
                                            ALU.add).then_inc(res_ready, 1)
                if n >= 1:
                    o = n - 1
                    mo = batch(o)
                    qo = o % 2
                    dve.wait_ge(stdf_ready, n)
                    nc.vector.reciprocal(rstdf[:, qo, 0:mo], stdf[:, qo, 0:mo]).then_inc(rstdf_ready, 1)
                if n < NQ:
                    dve.wait_ge(res_ready, n + 1)
                    for j in range(m):
                        ins = nc.vector.bn_stats(stf[:, q, j, :], res[:, q, j, :])
                    ins.then_inc(stf_ready, 1)
                if n >= 1:
                    dve.wait_ge(rstdf_ready, n)
                    nc.vector.scalar_tensor_tensor(nbias[:, qo, 0:mo], mvf[:, qo, 0:mo, 0], -1.0, rstdf[:, qo, 0:mo],
                                                   op0=ALU.mult, op1=ALU.mult).then_inc(nbias_ready, 1)
                if n < NQ:
                    dve.wait_ge(stf_ready, n + 1)
                    for j in range(m):
                        ins = nc.vector.bn_aggr(mvf[:, q, j, :], stf[:, q, j, :])
                    ins.then_inc(mvf_ready, 1)


_INS = ["x", "src", "dst", "edge_weight", "L0_gnn_w1", "L0_gnn_b1", "L0_gnn_g1", "L0_gnn_be1",
        "L0_gnn_w2", "L0_gnn_b2", "L0_gnn_g2", "L0_gnn_be2"]


def kernel(**inputs):
    import numpy as _np
    import concourse.bacc as _bacc
    from concourse.bass_utils import run_bass_kernel_spmd as _run

    nc = _bacc.Bacc("TRN2", target_bir_lowering=False, num_devices=1)
    arrays, args = {}, []
    for name in _INS:
        a = _np.ascontiguousarray(inputs[name])
        arrays[f"in_{name}"] = a
        args.append(nc.dram_tensor(f"in_{name}", a.shape, mybir.dt.from_np(a.dtype), kind="ExternalInput").ap())
    shape = inputs["x"].shape
    args.append(nc.dram_tensor("out_0", shape, F32, kind="ExternalOutput").ap())
    gnn_layer(nc, *args)
    r = _run(nc, [arrays], core_ids=[0])
    return r.results[0]["out_0"]
```

```python
from contextlib import ExitStack

import concourse.bass as bass
from concourse import mybir

F32 = mybir.dt.float32
BF16 = mybir.dt.bfloat16
I32 = mybir.dt.int32
I16 = mybir.dt.int16
ALU = mybir.AluOpType
ACT = mybir.ActivationFunctionType
AX = mybir.AxisListType

P = 128
C = 128
T = 4
GE = T * P
K = 4
W = 64
HOP = 32
MARGIN = 16
SPAN = HOP * (K - 1) + W
WIDE = 512
EPS = 1e-5
SLOPE = 0.2


def gnn_layer(nc, x, src, dst, ew, w1, b1, g1, be1, w2, b2, g2, be2, out):
    N = x.shape[0]
    E = src.shape[0]
    SE = K * GE
    S = (E + SE - 1) // SE
    G = S * K
    NT = G * T
    IB = 7
    BT = NT // IB
    HB = ((0, 4), (4, IB))
    NN = (N + P - 1) // P
    NL = N - (NN - 1) * P
    NQ = (NN + 3) // 4
    NB = 4
    XL = [0, 4, 12, 24, 36, NN]
    ROWS = (MARGIN + N + SPAN + P - 1) // P * P
    NW = (N + WIDE - 1) // WIDE
    FT = E // P
    RE = E - FT * P
    rest_e = E % SE
    own_e = rest_e - (K - 1) * GE
    dst_pieces = 1 if rest_e == 0 else 2 + -(-(SE - rest_e) // own_e)
    assert BT * IB == NT and BT <= P and S <= P and G % 2 == 0
    assert rest_e == 0 or own_e > 0
    assert RE > 0 and (IB - 1) * BT < FT < NT

    ctx = ExitStack()
    with ctx:
        def sb(name, shape, dt):
            return ctx.enter_context(nc.sbuf_tensor(name, shape, dt))

        def psum(name, shape, dt=F32):
            return ctx.enter_context(nc.psum_tensor(name, shape, dt))

        def sem(name):
            return ctx.enter_context(nc.semaphore(name))

        def sems(name, n=K):
            return [sem(f"{name}{k}") for k in range(n)]

        src_table = nc.dram_tensor("src_table", (NN * P, C), F32, kind="Internal").ap()
        dst_table = nc.dram_tensor("dst_table", (ROWS, 3 * C), BF16, kind="Internal").ap()
        dst16_dram = nc.dram_tensor("dst16_dram", (NT * P,), I16, kind="Internal").ap()

        W1S, W1D, W2, B1, B2 = range(5)
        raw = sb("raw", [P, 5, C], F32)
        mid = sb("mid", [P, 5, C], F32)
        raw_st = sb("raw_st", [P, 5, 6], F32)
        raw_mv = sb("raw_mv", [P, 5, 2], F32)
        b_part = sb("b_part", [P, 2, 3, C], BF16)
        b_rest = sb("b_rest", [P, 2, C], F32)
        b1_rows = sb("b1_rows", [P, 4, C], BF16)
        b2_rows = sb("b2_rows", [P, 4, C], BF16)
        g2_bc = sb("g2_bc", [P, C], F32)
        be2_bc = sb("be2_bc", [P, T, C], F32)
        g1_col = sb("g1_col", [P, 1], F32)
        be1_col = sb("be1_col", [P, 1], F32)
        eps_col = sb("eps_col", [P, 1], F32)
        ones_bf = sb("ones_bf", [P, P], BF16)
        ones_f = sb("ones_f", [P, P], F32)
        ident = sb("ident", [P, P], F32)
        ident_bf = sb("ident_bf", [P, P], BF16)
        iota_row = sb("iota_row", [P, W], F32)
        iota_col = sb("iota_col", [W, 1], F32)
        iota_wide = sb("iota_wide", [P, WIDE], F32)
        wide_off = sb("wide_off", [P, NW], F32)
        win_off = sb("win_off", [P, K], F32)
        zero_bf = sb("zero_bf", [P, 3 * C], BF16)

        src_t = sb("src_t", [BT, IB, P], I32)
        dst_t = sb("dst_t", [BT, IB, P], I32)
        ew_t = sb("ew_t", [BT, IB, P], F32)
        src_tf = sb("src_tf", [BT, IB, P], F32)
        dst_tf = sb("dst_tf", [BT, IB, P], F32)
        dst16_t = sb("dst16_t", [BT, IB, P], I16)
        src_idx = sb("src_idx", [P, NT + 2 * T], I32)
        dst_idx = sb("dst_idx", [P, NT + 2 * T], I32)
        dst_f = sb("dst_f", [P, NT], F32)
        ew_all = sb("ew_all", [P, NT], F32)
        dst_rel = sb("dst_rel", [P, S, K, T], F32)
        dst_s = sb("dst_s", [S, K, GE], I32)
        dst_min = sb("dst_min", [S, K], F32)
        dst_max = sb("dst_max", [S, K], F32)
        miss = sb("miss", [S, 2, K], F32)
        base_col = sb("base_col", [S, 1], F32)
        base_diag = sb("base_diag", [S, S + 1], F32)
        base_bc = sb("base_bc", [P, S], F32)
        base_i = sb("base_i", [1, S + 1], I32)
        win_node = sb("win_node", [W, S, K], F32)

        x_all = sb("x_all", [P, NN, C], F32)
        tab_src = sb("tab_src", [P, NB, 4, C], F32)
        tab_dst = sb("tab_dst", [P, NB, 4, 3, C], BF16)
        tab_rest = sb("tab_rest", [P, 2, 4, C], F32)
        ACOLS = max(ROWS, MARGIN + NW * WIDE)
        acc = sb("acc", [P, ACOLS], F32)

        idx_slot = sb("idx_slot", [P, 2, 2 * T], I32)
        a_src = sb("a_src", [P, K, T, C], F32)
        dst_bc = sb("dst_bc", [W, K, GE], I16)
        pick = sb("pick", [W, 2, GE], BF16)
        win = sb("win", [W, K, 3, C], BF16)
        junk = sb("junk", [P, 2, 2, T, C], BF16)
        ssq = sb("ssq", [P, 2, 2, T], F32)
        std = sb("std", [P, 2, 2, T], F32)
        rstd = sb("rstd", [P, 2, 2, T], F32)
        cn = sb("cn", [P, 2, T, C], F32)
        aff = sb("aff", [P, 2, GE], F32)
        z = sb("z", [P, 2, GE], F32)
        t2 = sb("t2", [P, T, C], F32)
        u2 = sb("u2", [P, T, C], F32)
        y = sb("y", [P, K, T, C], F32)
        seg = sb("seg", [P, K, T, W], F32)

        idx2_slot = sb("idx2_slot", [P, 2, T], I32)
        b_dst = sb("b_dst", [P, T, 3 * C], BF16)
        seg_wide = sb("seg_wide", [P, T, WIDE], F32)

        stf = sb("stf", [P, 2, 4, 6], F32)
        mvf = sb("mvf", [P, 2, 4, 2], F32)
        stdf = sb("stdf", [P, 2, 4], F32)
        rstdf = sb("rstdf", [P, 2, 4], F32)
        nbias = sb("nbias", [P, 2, 4], F32)
        fin = sb("fin", [P, NB, 4, C], F32)

        ps_c = [psum(f"ps_c{b}", [P, T, C]) for b in range(2)]
        ps_cT = psum("ps_cT", [P, GE])
        ps_h = [psum(f"ps_h{b}", [P, T, C]) for b in range(2)]
        ps_o = psum("ps_o", [P, 512])
        ps_t = [psum(f"ps_t{b}", [P, 512]) for b in range(2)]

        last_banks = ps_c + ps_h

        w_in = sem("w_in")
        v_in = sem("v_in")
        src_in = sem("src_in")
        dst_in = sem("dst_in")
        ew_in = sem("ew_in")
        dsts_in = sem("dsts_in")
        x_in = sems("x_in", len(XL) - 1)
        x_tail_in = sem("x_tail_in")
        zero_ok = sem("zero_ok")
        ident_ok = sem("ident_ok")
        const_ok = sem("const_ok")
        dve_own = sem("dve_own")
        centred = sem("centred")
        b_split = sem("b_split")
        src_cast = sem("src_cast")
        dst_cast = sem("dst_cast")
        dst16_cast = sem("dst16_cast")
        turned = sem("turned")
        turn_out = sem("turn_out")
        base_set = sem("base_set")
        base_ps = sem("base_ps")
        base_ok = sem("base_ok")
        rel_ok = sem("rel_ok")
        dst16_out = sem("dst16_out")
        zero_out = sem("zero_out")
        node_T = sem("node_T")
        node_Tc = sem("node_Tc")
        node_A = sem("node_A")
        node_Ac = sem("node_Ac")
        node_B = sem("node_B")
        node_hi = sem("node_hi")
        node_r1 = sem("node_r1")
        node_mid = sem("node_mid")
        node_lo = sem("node_lo")
        src_out = sems("src_out", NB)
        tab_out = sems("tab_out", NB)

        idx_in = sems("idx_in", 2)
        gathered = sems("gathered")
        gathers_begun = sem("gathers_begun")
        dstbc_in = sems("dstbc_in", 2)
        win_in = sems("win_in", 2)
        pick_ready = sems("pick_ready")
        c_ready = sems("c_ready")
        ssq1_ready = sems("ssq1_ready")
        std_ready = sems("std_ready")
        rstd_ready = sems("rstd_ready")
        cn_ready = sems("cn_ready")
        cT_ready = sems("cT_ready")
        aff_ready = sems("aff_ready")
        z_ready = sems("z_ready")
        h_ready = sems("h_ready")
        ssq2_ready = sems("ssq2_ready")
        t2_ready = sems("t2_ready")
        u2_ready = sems("u2_ready")
        y_ready = sems("y_ready")
        onehot_ready = sems("onehot_ready")
        o_ready = sem("o_ready")
        acc_done = sem("acc_done")

        gen_idx = sems("gen_idx", 2)
        gen_gathered = sems("gen_gathered", 2)
        gen = {name: sem("gen_" + name) for name in (
            "c", "ssq1", "std1", "rstd1", "cn", "cT", "aff", "z", "h", "ssq2", "std2", "rstd2", "t2", "u2",
            "y", "seg", "o", "acc")}

        sums_done = sem("sums_done")
        fT_ready = sem("fT_ready")
        stf_ready = sem("stf_ready")
        mvf_ready = sem("mvf_ready")
        stdf_ready = sem("stdf_ready")
        rstdf_ready = sem("rstdf_ready")
        nbias_ready = sem("nbias_ready")
        fin_ready = sem("fin_ready")
        out_done = sems("out_done", NB)

        block = ctx.enter_context(nc.Block())

        def live(s, k, lag):
            if isinstance(s, int):
                return 0 <= K * s + k - lag < G
            return True

        class Back:

            def __init__(self, counts, k, lag):
                self.slot = (k - lag) % K
                self.buf = self.slot % 2
                self.count = counts[(k - lag) // K]

        HEAD = 2

        def supersteps(eng, step):
            for s in range(HEAD):
                step(s, {0: s + 1, -1: s, -2: s - 1})
            with eng.Fori(HEAD, S) as s:
                step(s, {0: eng.snap(s + 1), -1: s, -2: eng.snap(s - 1)})
            for s in range(S, S + HEAD):
                step(s, {0: s + 1, -1: s, -2: s - 1})

        def batch(n):
            return min(4, NN - 4 * n)

        def both_paths(eng, fast, general):
            eng.wait_ge(base_ok, 1)
            misses = eng.value_load(base_i[0:1, S:S + 1], min_val=0, max_val=2 * G)
            with eng.If(misses == 0):
                fast()
            with eng.Else():
                general()

        def act_sum_squares(which, junk_buf, bank, sums):
            for t in range(T):
                ins = nc.scalar.activation(junk[:, which, junk_buf, t, :], bank[:, t, :], ACT.Square,
                                           accum_out=sums[:, t:t + 1])
            return ins

        def act_std(b, a, z_):
            return nc.scalar.activation(std[:, b, a:z_, :], ssq[:, b, a:z_, :], ACT.Sqrt, bias=eps_col[:, 0:1],
                                        scale=1.0 / C)

        def act_normalise(b, bank, rstds):
            for t in range(T):
                ins = nc.scalar.activation(cn[:, b, t, :], bank[:, t, :], ACT.Copy, scale=rstds[:, t:t + 1])
            return ins

        def act_affine(b):
            return nc.scalar.activation(aff[:, b, :], ps_cT[:], ACT.Identity, bias=be1_col[:, 0:1],
                                        scale=g1_col[:, 0:1])

        def pe_source_rows(bank, slot):
            nc.tensor.matmul(bank[:], ident[:], a_src[:, slot, :, :], start=True, stop=True)

        def pe_turn(b):
            for t in range(T):
                mm = nc.tensor.transpose(ps_cT[:, t * P:(t + 1) * P], cn[:, b, t, :], ident[:])
            return mm

        def pe_second_product(b, bank):
            nc.tensor.matmul(bank[:], ones_bf[:], b2_rows[:], start=True, stop=True)
            for t in range(T):
                mm = nc.tensor.matmul(bank[:, t, :], z[:, b, t * P:(t + 1) * P], mid[:, W2, :],
                                      start=False, stop=True, skip_group_check=True)
            return mm

        def dve_leaky1(b):
            return nc.vector.scalar_tensor_tensor(z[:, b, :], aff[:, b, :], SLOPE, aff[:, b, :],
                                                  op0=ALU.mult, op1=ALU.max)

        def dve_scale2(bank, rstds):
            for t in range(T):
                ins = nc.vector.scalar_tensor_tensor(t2[:, t, :], bank[:, t, :], rstds[:, t:t + 1], g2_bc[:],
                                                     op0=ALU.mult, op1=ALU.mult)
            return ins

        def dve_shift2():
            return nc.vector.tensor_tensor(u2[:], t2[:], be2_bc[:], ALU.add)

        def dve_leaky2(slot):
            return nc.vector.scalar_tensor_tensor(y[:, slot, :, :], u2[:], SLOPE, u2[:], op0=ALU.mult, op1=ALU.max)

        def outs(n, q):
            total = 0
            for i in range(q, n, NB):
                m = batch(i)
                full = m if 4 * i + m < NN or NL == P else m - 1
                total += (full > 0) + (full < m)
            return total

        def uses(q):
            return (NQ - q + NB - 1) // NB

        @block.sync
        def _(sp):
            sp.dma_start(raw[:, W1S:W1D + 1, :], w1.rearrange("(h p) c -> p h c", p=P)).then_inc(w_in, 16)
            for i, (a, b) in enumerate(zip(XL[:-1], XL[1:])):
                b = min(b, NN - 1)
                sp.dma_start(x_all[:, a:b, :], x[a * P:b * P].rearrange("(n p) c -> p n c", p=P)).then_inc(x_in[i], 16)
            sp.wait_ge(zero_ok, 1)
            sp.dma_start(x_all[0:NL, NN - 1, :], x[(NN - 1) * P:N]).then_inc(x_tail_in, 16)
            for n in range(NQ):
                m = batch(n)
                sp.wait_ge(node_Ac, n + 1)
                sp.dma_start(src_table[4 * n * P:(4 * n + m) * P].rearrange("(t p) c -> p t c", p=P),
                             tab_src[:, n % NB, 0:m, :]).then_inc(src_out[n % NB], 16)
            sp.dma_start(g2_bc[:], g2.partition_broadcast(P)).then_inc(v_in, 16)
            for t in range(T):
                sp.dma_start(be2_bc[:, t, :], be2.partition_broadcast(P)).then_inc(v_in, 16)
            sp.dma_start(g1_col[:], g1.rearrange("(p o) -> p o", o=1)).then_inc(v_in, 16)
            sp.dma_start(be1_col[:], be1.rearrange("(p o) -> p o", o=1)).then_inc(v_in, 16)
            zeros = 0
            for r0, r1 in ((0, MARGIN), (MARGIN + NN * P, ROWS)):
                while r0 < r1:
                    n = min(P, r1 - r0)
                    sp.dma_start(dst_table[r0:r0 + n], zero_bf[0:n]).then_inc(zero_out, 16)
                    zeros += 1
                    r0 += n
            sp.wait_ge(dst16_cast, 1)
            sp.dma_start(dst16_dram.rearrange("(b p e) -> p b e", b=IB, e=P), dst16_t[:]).then_inc(dst16_out, 16)
            for n in range(NQ):
                m = batch(n)
                sp.wait_ge(node_lo, n + 1)
                r0 = MARGIN + 4 * n * P
                sp.dma_start(dst_table[r0:r0 + m * P].rearrange("(t p) c -> p t c", p=P),
                             tab_dst[:, n % NB, 0:m, :, :].rearrange("p t q c -> p t (q c)")).then_inc(tab_out[n % NB], 16)
            sp.wait_ge(zero_out, 16 * zeros)
            for q in range(NB):
                sp.wait_ge(tab_out[q], 16 * uses(q))
            sp.wait_ge(dst16_out, 16)

            def step(s, counts):
                first = isinstance(s, int)
                if first and s >= S:
                    return
                base = sp.value_load(base_i[0:1, bass.ds(s, 1)], min_val=0, max_val=N - 1)
                for h in range(2):
                    k0 = 2 * h
                    if not first or s > 0:
                        if first or h == 1:
                            sp.wait_ge(gathered[k0], counts[-1] * (16 * T))
                        sp.wait_ge(gathered[k0 + 1], counts[-1] * (16 * T))
                    if not first:
                        sp.snap(s + h)
                    at = s * (K * T) + k0 * T
                    sp.dma_start(idx_slot[:, h, :], src_idx[:, bass.ds(at, 2 * T)]).then_inc(idx_in[h], 16)
                    if not first or s > 0:
                        sp.wait_ge(pick_ready[k0 + 1], counts[-1])
                    at = s * SE + k0 * GE
                    sp.dma_start(dst_bc[:, k0:k0 + 2, :].rearrange("p k e -> p (k e)"),
                                 dst16_dram[bass.ds(at, 2 * GE)].partition_broadcast(W)).then_inc(dstbc_in[h], 16)
                    if not first or s > 0:
                        sp.wait_ge(c_ready[k0 + 1], counts[-1])
                    for k in (k0, k0 + 1):
                        sp.dma_start(win[:, k, :, :].rearrange("w q c -> w (q c)"),
                                     dst_table[bass.ds(base + HOP * k, W), :]).then_inc(win_in[h], 16)

            def general():
                sp.wait_ge(base_ok, 1)

            both_paths(sp, lambda: supersteps(sp, step), general)

            for n in range(NQ):
                m = batch(n)
                full = m if 4 * n + m < NN or NL == P else m - 1
                sp.wait_ge(fin_ready, n + 1)
                if full:
                    sp.dma_start(out[4 * n * P:(4 * n + full) * P].rearrange("(t p) c -> p t c", p=P),
                                 fin[:, n % NB, 0:full, :]).then_inc(out_done[n % NB], 16)
                if full < m:
                    sp.dma_start(out[(NN - 1) * P:N], fin[0:NL, n % NB, full, :]).then_inc(out_done[n % NB], 16)
            for q in range(NB):
                sp.wait_ge(out_done[q], 16 * outs(NQ, q))

        @block.gpsimd
        def _(pool):
            nc.gpsimd.memset(x_all[:, NN - 1, :], 0.0)
            nc.gpsimd.memset(src_t[:, IB - 1, :], 0)
            nc.gpsimd.memset(dst_t[:, IB - 1, :], 0)
            nc.gpsimd.memset(ew_t[:, IB - 1, :], 0.0).then_inc(zero_ok, 1)
            nc.gpsimd.memset(ident[:], 0.0).then_inc(ident_ok, 1)
            pool.wait_ge(ident_ok, 1)
            nc.gpsimd.affine_select(out=ident[:], in_=ident[:], compare_op=ALU.not_equal, fill=1.0, base=0,
                                    pattern=[[-1, P]], channel_multiplier=1).then_inc(ident_ok, 1)
            nc.gpsimd.memset(ones_f[:], 1.0)
            nc.gpsimd.memset(ones_bf[:], 1.0)
            nc.gpsimd.memset(eps_col[:], EPS)
            nc.gpsimd.memset(b1_rows[:], 0.0)
            nc.gpsimd.memset(b2_rows[:], 0.0)
            nc.gpsimd.memset(zero_bf[:], 0.0)
            nc.gpsimd.memset(src_idx[:, NT:NT + 2 * T], 0)
            nc.gpsimd.memset(dst_idx[:, NT:NT + 2 * T], 0)
            nc.gpsimd.memset(acc[:, 0:MARGIN], 0.0)
            nc.gpsimd.memset(acc[:, MARGIN + NN * P:ACOLS], 0.0)
            nc.gpsimd.iota(iota_row[:], [[1, W]], base=0, channel_multiplier=0,
                           allow_small_or_imprecise_dtypes=True)
            nc.gpsimd.iota(iota_wide[:], [[1, WIDE]], base=0, channel_multiplier=0,
                           allow_small_or_imprecise_dtypes=True)
            nc.gpsimd.iota(wide_off[:], [[WIDE, NW]], base=0, channel_multiplier=0,
                           allow_small_or_imprecise_dtypes=True)
            nc.gpsimd.iota(win_off[:], [[HOP, K]], base=-MARGIN, channel_multiplier=0,
                           allow_small_or_imprecise_dtypes=True)
            nc.gpsimd.iota(iota_col[:], [[0, 1]], base=0, channel_multiplier=1,
                           allow_small_or_imprecise_dtypes=True).then_inc(const_ok, 1)
            for q in range(NB):
                pool.wait_ge(src_out[q], 16 * uses(q))

            def gather(dest, table, index, done):
                nc.gpsimd.indirect_dma_start(out=dest, out_offset=None, in_=table,
                                             in_offset=bass.IndirectOffsetOnAxis(ap=index, axis=0)).then_inc(done, 16)

            def step(s, counts):
                first = isinstance(s, int)
                if first and s >= S:
                    return
                for k in range(K):
                    if k % 2 == 0:
                        pool.wait_ge(idx_in[k // 2], counts[0] * 16)
                    if not first or s > 0:
                        pool.wait_ge(c_ready[k], counts[-1])
                    pool.sem_inc(gathers_begun, 1)
                    for t in range(T):
                        gather(a_src[:, k, t, :], src_table, idx_slot[:, k // 2, (k % 2) * T + t:(k % 2) * T + t + 1],
                               gathered[k])

            def general():
                pool.wait_ge(turn_out, 6)
                for q in range(NB):
                    pool.wait_ge(tab_out[q], 16 * uses(q))
                nc.gpsimd.tensor_copy(idx_slot[:, 0, 0:T], src_idx[:, 0:T])
                nc.gpsimd.tensor_copy(idx2_slot[:, 0, :], dst_idx[:, 0:T]).then_inc(gen_idx[0], 1)
                with pool.Fori(0, G // 2) as i:
                    n = pool.snap(i + 1)
                    for b in range(2):
                        before = pool.snap(i * (2 * NW) + (b * NW + 1))
                        pool.wait_ge(gen_idx[b], n)
                        pool.wait_ge(gen["acc"], before)
                        at = i * (2 * T) + (b + 1) * T
                        nc.gpsimd.tensor_copy(idx_slot[:, 1 - b, 0:T], src_idx[:, bass.ds(at, T)])
                        nc.gpsimd.tensor_copy(idx2_slot[:, 1 - b, :], dst_idx[:, bass.ds(at, T)]).then_inc(gen_idx[1 - b], 1)
                        for t in range(T):
                            gather(a_src[:, 0, t, :], src_table, idx_slot[:, b, t:t + 1], gen_gathered[b])
                            gather(b_dst[:, t, :], dst_table, idx2_slot[:, b, t:t + 1], gen_gathered[b])

            both_paths(pool, lambda: supersteps(pool, step), general)

        @block.scalar
        def _(act):
            def tiles_in(dest, dram, done):
                full = (IB - 1) * BT
                act.dma_start(dest[:, 0:IB - 1, :],
                              dram[0:full * P].rearrange("(b p e) -> p b e", b=IB - 1, e=P)).then_inc(done, 16)
                act.wait_ge(zero_ok, 1)
                act.dma_start(dest[0:FT - full, IB - 1, :],
                              dram[full * P:FT * P].rearrange("(p e) -> p e", e=P)).then_inc(done, 16)
                act.dma_start(dest[FT - full:FT - full + 1, IB - 1, 0:RE],
                              dram[FT * P:E].rearrange("(p e) -> p e", p=1)).then_inc(done, 16)

            act.dma_start(raw[:, B1, :], b1.partition_broadcast(P)).then_inc(w_in, 16)
            act.dma_start(raw[:, W2, :], w2).then_inc(w_in, 16)
            act.dma_start(raw[:, B2, :], b2.partition_broadcast(P)).then_inc(w_in, 16)
            full = E // SE
            act.dma_start(dst_s[0:full], dst[0:full * SE].rearrange("(s k e) -> s k e", k=K, e=GE)).then_inc(dsts_in, 16)
            if rest_e:
                row = dst_s[full:full + 1].rearrange("s k e -> s (k e)")
                act.dma_start(row[:, 0:rest_e], dst[full * SE:E].rearrange("(s e) -> s e", s=1)).then_inc(dsts_in, 16)
                at = rest_e
                while at < SE:
                    n = min(own_e, SE - at)
                    act.dma_start(row[:, at:at + n], dst[E - n:E].rearrange("(s e) -> s e", s=1)).then_inc(dsts_in, 16)
                    at += n
            tiles_in(src_t, src, src_in)
            tiles_in(dst_t, dst, dst_in)
            tiles_in(ew_t, ew, ew_in)

            for n in range(NQ):
                m = batch(n)
                act.wait_ge(node_T, n + 1)
                at = MARGIN + 4 * n * P
                nc.scalar.copy(acc[:, at:at + m * P], ps_t[n % 2][:, 0:m * P]).then_inc(node_Tc, 1)
                if n == 6:
                    act.wait_ge(src_in, 48)
                    nc.scalar.copy(src_tf[:], src_t[:]).then_inc(src_cast, 1)
                if n == 8:
                    act.wait_ge(dst_in, 48)
                    nc.scalar.copy(dst16_t[:], dst_t[:]).then_inc(dst16_cast, 1)
                if n == 10:
                    nc.scalar.copy(dst_tf[:], dst_t[:]).then_inc(dst_cast, 1)

            for n in range(NQ + 1):
                if n < NQ:
                    m = batch(n)
                    act.wait_ge(node_B, n + 1)
                    if n >= NB:
                        act.wait_ge(tab_out[n % NB], 16 * (n // NB))
                    nc.scalar.copy(tab_dst[:, n % NB, 0:m, 0, :], ps_c[n % 2][:, 0:m, :]).then_inc(node_hi, 1)
                if n >= 1:
                    o = n - 1
                    m = batch(o)
                    act.wait_ge(node_r1, o + 1)
                    nc.scalar.copy(tab_dst[:, o % NB, 0:m, 1, :], tab_rest[:, o % 2, 0:m, :]).then_inc(node_mid, 1)
            act.wait_ge(v_in, 16 * 7)

            def step(s, counts):
                for k in range(K):
                    b = k % 2
                    g2_, g3, g5 = (Back(counts, k, lag) for lag in (2, 3, 5))
                    norm1, norm2 = live(s, k, 2), live(s, k, 5)
                    if norm2:
                        act.wait_ge(h_ready[g5.slot], g5.count)
                        act_sum_squares(1, g5.buf, ps_h[g5.buf], ssq[:, b, 1, :]).then_inc(ssq2_ready[g5.slot], 1)
                    if norm1 or norm2:
                        if norm1:
                            act.wait_ge(ssq1_ready[g2_.slot], g2_.count)
                        if norm2:
                            act.wait_ge(ssq2_ready[g5.slot], g5.count)
                        act_std(b, 0 if norm1 else 1, 2 if norm2 else 1).then_inc(std_ready[g2_.slot], 1)
                    if live(s, k, 3):
                        act.wait_ge(cT_ready[g3.slot], g3.count)
                        act_affine(g3.buf).then_inc(aff_ready[g3.slot], 1)
                    if norm1:
                        act.wait_ge(rstd_ready[g2_.slot], g2_.count)
                        act_normalise(g2_.buf, ps_c[g2_.buf], rstd[:, b, 0, :]).then_inc(cn_ready[g2_.slot], 1)
                    if live(s, k, 1):
                        g = Back(counts, k, 1)
                        act.wait_ge(c_ready[g.slot], g.count)
                        act_sum_squares(0, g.buf, ps_c[g.buf], ssq[:, 1 - b, 0, :]).then_inc(ssq1_ready[g.slot], 1)

            def general():
                with act.Fori(0, G) as g:
                    n = act.snap(g + 1)
                    act.wait_ge(gen["c"], n)
                    act_sum_squares(0, 0, ps_c[0], ssq[:, 0, 0, :]).then_inc(gen["ssq1"], 1)
                    act.wait_ge(gen["ssq1"], n)
                    act_std(0, 0, 1).then_inc(gen["std1"], 1)
                    act.wait_ge(gen["rstd1"], n)
                    act_normalise(0, ps_c[0], rstd[:, 0, 0, :]).then_inc(gen["cn"], 1)
                    act.wait_ge(gen["cT"], n)
                    act_affine(0).then_inc(gen["aff"], 1)
                    act.wait_ge(gen["h"], n)
                    act_sum_squares(1, 0, ps_h[0], ssq[:, 0, 1, :]).then_inc(gen["ssq2"], 1)
                    act.wait_ge(gen["ssq2"], n)
                    act_std(0, 1, 2).then_inc(gen["std2"], 1)

            both_paths(act, lambda: supersteps(act, step), general)

            for n in range(NQ + 1):
                if n < NQ:
                    m = batch(n)
                    act.wait_ge(mvf_ready, n + 1)
                    nc.scalar.activation(stdf[:, n % 2, 0:m], mvf[:, n % 2, 0:m, 1], ACT.Sqrt,
                                         bias=eps_col[:, 0:1]).then_inc(stdf_ready, 1)
                if n >= 1:
                    o = n - 1
                    q = o % 2
                    m = batch(o)
                    act.wait_ge(nbias_ready, n)
                    if o >= NB:
                        act.wait_ge(out_done[o % NB], 16 * outs(o, o % NB))
                    for j in range(m):
                        ins = nc.scalar.activation(fin[:, o % NB, j, :], last_banks[o % 4][:, j, :], ACT.Identity,
                                                   bias=nbias[:, q, j:j + 1], scale=rstdf[:, q, j:j + 1])
                    ins.then_inc(fin_ready, 1)

        @block.tensor
        def _(pe):
            def turn_indices(q, tile_rows, cast, done):
                pe.wait_ge(cast, done)
                for half, (b0, b1_) in enumerate(HB):
                    if q:
                        pe.wait_ge(turn_out, 2 * (q - 1) + half + 1)
                    bank = (ps_cT, ps_o)[half]
                    for blk in range(b0, b1_):
                        at = (blk - b0) * BT
                        mm = nc.tensor.transpose(bank[:, at:at + BT], tile_rows[:, blk, :], ident[0:BT, 0:BT])
                    mm.then_inc(turned, 1)

            def node_turn(n):
                m = batch(n)
                for i, a in enumerate(XL[:-1]):
                    if 4 * n + m > a:
                        pe.wait_ge(x_in[i], 16)
                if n == NQ - 1:
                    pe.wait_ge(x_tail_in, 16)
                if n >= 2:
                    pe.wait_ge(node_Tc, n - 1)
                for j in range(m):
                    mm = nc.tensor.transpose(ps_t[n % 2][:, j * P:(j + 1) * P], x_all[:, 4 * n + j, :], ident[:])
                mm.then_inc(node_T, 1)

            def product(n, w, bank, start):
                for j in range(batch(n)):
                    at = MARGIN + (4 * n + j) * P
                    mm = nc.tensor.matmul(bank[:, j, :], acc[:, at:at + P], mid[:, w, :], start=start, stop=True,
                                          skip_group_check=True)
                return mm

            pe.wait_ge(ident_ok, 2)
            node_turn(0)
            node_turn(1)
            pe.wait_ge(centred, 1)
            for n in range(NQ):
                pe.wait_ge(node_Tc, n + 1)
                if n >= 2:
                    pe.wait_ge(node_Ac, n - 1)
                product(n, W1S, ps_h[n % 2], True).then_inc(node_A, 1)
                if n + 2 < NQ:
                    node_turn(n + 2)
                if n == 9:
                    turn_indices(0, src_tf, src_cast, 1)
                if n == NQ - 1:
                    pe.wait_ge(base_set, 1)
                    pe.wait_ge(turn_out, 2)
                    nc.tensor.matmul(ps_o[:, 0:S + 1], ones_f[0:S, :], base_diag[:], start=True,
                                     stop=True).then_inc(base_ps, 1)
            pe.wait_ge(b_split, 1)
            pe.wait_ge(base_ok, 1)
            for n in range(NQ):
                if n >= 2:
                    pe.wait_ge(node_r1, n - 1)
                nc.tensor.matmul(ps_c[n % 2][:, 0:batch(n), :], ones_bf[:], b1_rows[:, 0:batch(n), :], start=True,
                                 stop=True)
                product(n, W1D, ps_c[n % 2], False).then_inc(node_B, 1)
                if n == 1:
                    turn_indices(1, dst_tf, dst_cast, 1)
                if n == 4:
                    turn_indices(2, ew_t, ew_in, 48)
            pe.wait_ge(node_r1, NQ)
            pe.wait_ge(node_Ac, NQ)
            pe.wait_ge(turn_out, 6)
            pe.wait_ge(rel_ok, 1)
            pe.wait_ge(b_split, 2)

            def step(s, counts):
                for k in range(K):
                    if live(s, k, 3):
                        g = Back(counts, k, 3)
                        pe.wait_ge(cn_ready[g.slot], g.count)
                        if live(s, k, 4):
                            g4 = Back(counts, k, 4)
                            pe.wait_ge(aff_ready[g4.slot], g4.count)
                        pe_turn(g.buf).then_inc(cT_ready[g.slot], 1)
                    if live(s, k, 4):
                        g = Back(counts, k, 4)
                        if live(s, k, 6):
                            g6 = Back(counts, k, 6)
                            pe.wait_ge(t2_ready[g6.slot], g6.count)
                        pe.wait_ge(z_ready[g.slot], g.count)
                        pe_second_product(g.buf, ps_h[g.buf]).then_inc(h_ready[g.slot], 1)
                    if live(s, k, 1):
                        g = Back(counts, k, 1)
                        if live(s, k, 3):
                            g3 = Back(counts, k, 3)
                            pe.wait_ge(cn_ready[g3.slot], g3.count)
                        pe.wait_ge(gathered[g.slot], g.count * (16 * T))
                        pe_source_rows(ps_c[g.buf], g.slot)
                        pe.wait_ge(pick_ready[g.slot], g.count)
                        pe.wait_ge(win_in[g.slot // 2], g.count * 32)
                        for t in range(T):
                            for part in range(3):
                                mm = nc.tensor.matmul(ps_c[g.buf][:, t, :], pick[:, g.buf, t * P:(t + 1) * P],
                                                      win[:, g.slot, part, :], start=False, stop=True,
                                                      skip_group_check=True)
                        mm.then_inc(c_ready[g.slot], 1)
                    if live(s, k, 6):
                        g = Back(counts, k, 6)
                        pe.wait_ge(y_ready[g.slot], g.count)
                        if g.slot == 0:
                            pe.wait_ge(acc_done, g.count)
                        at = HOP * g.slot
                        for t in range(T):
                            mm = nc.tensor.matmul(ps_o[:, at:at + W], y[:, g.slot, t, :], seg[:, g.slot, t, :],
                                                  start=(g.slot == 0 and t == 0), stop=True, skip_group_check=True)
                        if g.slot == K - 1:
                            mm.then_inc(o_ready, 1)

            def general():
                with pe.Fori(0, G // 2) as i:
                    for b in range(2):
                        n = pe.snap(2 * i + (b + 1))
                        pe.wait_ge(gen_gathered[b], (i + 1) * (16 * 2 * T))
                        pe_source_rows(ps_c[0], 0)
                        for part in range(3):
                            mm = nc.tensor.matmul(ps_c[0][:], ident_bf[:], b_dst[:, :, part * C:(part + 1) * C], start=False,
                                                  stop=True, skip_group_check=True)
                        mm.then_inc(gen["c"], 1)
                        pe.wait_ge(gen["cn"], n)
                        pe_turn(0).then_inc(gen["cT"], 1)
                        pe.wait_ge(gen["z"], n)
                        pe_second_product(0, ps_h[0]).then_inc(gen["h"], 1)
                        with pe.Fori(0, NW) as w:
                            pe.wait_ge(gen["seg"], i * (2 * NW) + w + (b * NW + 1))
                            for t in range(T):
                                mm = nc.tensor.matmul(ps_o[:], y[:, 0, t, :], seg_wide[:, t, :],
                                                      start=(t == 0), stop=(t == T - 1))
                            mm.then_inc(gen["o"], 1)

            both_paths(pe, lambda: supersteps(pe, step), general)

            pe.wait_ge(sums_done, 1)
            for n in range(NQ):
                m = batch(n)
                if n >= 4:
                    pe.wait_ge(fin_ready, n - 3)
                for j in range(m):
                    at = MARGIN + (4 * n + j) * P
                    mm = nc.tensor.transpose(last_banks[n % 4][:, j, :], acc[:, at:at + P], ident[:])
                mm.then_inc(fT_ready, 1)

        @block.vector
        def _(dve):
            own = [0]

            def then(ins):
                own[0] += 1
                ins.then_inc(dve_own, 1)
                dve.wait_ge(dve_own, own[0])

            dve.wait_ge(w_in, 64)
            for i in range(5):
                ins = nc.vector.bn_stats(raw_st[:, i, :], raw[:, i, :])
            then(ins)
            for i in range(5):
                ins = nc.vector.bn_aggr(raw_mv[:, i, :], raw_st[:, i, :])
            then(ins)
            for i in range(5):
                ins = nc.vector.tensor_scalar(mid[:, i, :], raw[:, i, :], raw_mv[:, i, 0:1], None, ALU.subtract)
            ins.then_inc(centred, 1)
            dve.wait_ge(centred, 1)

            dve.wait_ge(const_ok, 1)
            for i, (b_bc, rows) in enumerate(((mid[:, B1, :], b1_rows), (mid[:, B2, :], b2_rows))):
                then(nc.vector.tensor_copy(b_part[:, i, 0, :], b_bc))
                then(nc.vector.tensor_tensor(b_rest[:, i, :], b_bc, b_part[:, i, 0, :], ALU.subtract))
                then(nc.vector.tensor_copy(b_part[:, i, 1, :], b_rest[:, i, :]))
                then(nc.vector.tensor_tensor(b_part[:, i, 2, :], b_rest[:, i, :], b_part[:, i, 1, :], ALU.subtract))
                for part in range(3):
                    r = 32 * part
                    ins = nc.vector.tensor_copy(rows[r:r + 1, :, :],
                                                b_part[r:r + 1, i, part, :].unsqueeze(1).to_broadcast([1, 4, C]))
                ins.then_inc(b_split, 1)

            def evacuate(q, half, *dests):
                dve.wait_ge(turned, 2 * q + half + 1)
                b0, b1_ = HB[half]
                for dest, shift in dests:
                    view = dest[:, b0 * BT:b1_ * BT]
                    bank = (ps_cT, ps_o)[half][:, 0:(b1_ - b0) * BT]
                    if shift:
                        ins = nc.vector.tensor_scalar(view, bank, float(shift), None, ALU.add)
                    else:
                        ins = nc.vector.tensor_copy(view, bank)
                ins.then_inc(turn_out, 1)

            def table_rest(n):
                m = batch(n)
                dve.wait_ge(node_hi, n + 1)
                if n >= 2:
                    dve.wait_ge(node_lo, n - 1)
                nc.vector.tensor_tensor(tab_rest[:, n % 2, 0:m, :], ps_c[n % 2][:, 0:m, :],
                                        tab_dst[:, n % NB, 0:m, 0, :], ALU.subtract).then_inc(node_r1, 1)

            def table_low(n):
                m = batch(n)
                dve.wait_ge(node_mid, n + 1)
                nc.vector.tensor_tensor(tab_dst[:, n % NB, 0:m, 2, :], tab_rest[:, n % 2, 0:m, :],
                                        tab_dst[:, n % NB, 0:m, 1, :], ALU.subtract).then_inc(node_lo, 1)

            def least_targets():
                dve.wait_ge(dsts_in, 16 * dst_pieces)
                nc.vector.tensor_reduce(dst_max[:], dst_s[:], AX.X, ALU.max)
                then(nc.vector.tensor_reduce(dst_min[:], dst_s[:], AX.X, ALU.min))
                then(nc.vector.tensor_reduce(base_col[:], dst_min[:], AX.X, ALU.min))
                dve.wait_ge(ident_ok, 2)
                nc.vector.tensor_scalar(base_diag[:, 0:S], ident[0:S, 0:S], base_col[:, 0:1], None, ALU.mult)
                for i, lim in enumerate((dst_min, dst_max)):
                    ins = nc.vector.scalar_tensor_tensor(miss[:, i, :], lim[:], base_col[:, 0:1], win_off[0:S, :],
                                                         op0=ALU.subtract, op1=ALU.subtract)
                then(ins)
                nc.vector.tensor_scalar(miss[:, 0, :], miss[:, 0, :], 0.0, None, ALU.is_lt)
                then(nc.vector.tensor_scalar(miss[:, 1, :], miss[:, 1, :], float(W - 1), None, ALU.is_gt))
                nc.vector.tensor_reduce(base_diag[:, S:S + 1], miss[:].rearrange("s i k -> s (i k)"), AX.X,
                                        ALU.add).then_inc(base_set, 1)

            def windows():
                then(nc.vector.tensor_tensor(dst_rel[:].rearrange("p s k t -> p s (k t)"),
                                             dst_f[:].rearrange("p (s m) -> p s m", s=S),
                                             base_bc[:].unsqueeze(2).to_broadcast([P, S, K * T]), ALU.subtract))
                for k in range(K):
                    off = float(HOP * k - MARGIN)
                    nc.vector.tensor_scalar(dst_rel[:, :, k, :], dst_rel[:, :, k, :], off, None, ALU.subtract)
                    ins = nc.vector.tensor_scalar(win_node[:, :, k], base_bc[0:W], iota_col[:, 0:1], off, ALU.add, ALU.add)
                ins.then_inc(rel_ok, 1)

            least_targets()
            nc.vector.tensor_copy(ident_bf[:], ident[:])
            for n in range(NQ):
                m = batch(n)
                dve.wait_ge(node_A, n + 1)
                if n >= NB:
                    dve.wait_ge(src_out[n % NB], 16 * (n // NB))
                nc.vector.tensor_copy(tab_src[:, n % NB, 0:m, :], ps_h[n % 2][:, 0:m, :]).then_inc(node_Ac, 1)
            evacuate(0, 0, (src_idx, 0))
            evacuate(0, 1, (src_idx, 0))
            dve.wait_ge(base_ps, 1)
            nc.vector.tensor_copy(base_bc[:], ps_o[:, 0:S])
            nc.vector.tensor_copy(base_i[:], ps_o[0:1, 0:S + 1]).then_inc(base_ok, 1)
            dve.wait_ge(base_ok, 1)
            for n in range(NQ):
                table_rest(n)
                if n >= 1:
                    table_low(n - 1)
                if n == 3:
                    evacuate(1, 0, (dst_f, 0), (dst_idx, MARGIN))
                    evacuate(1, 1, (dst_f, 0), (dst_idx, MARGIN))
                if n == 6:
                    evacuate(2, 0, (ew_all, 0))
                    evacuate(2, 1, (ew_all, 0))
                if n == 8:
                    windows()
            table_low(NQ - 1)
            dve.wait_ge(v_in, 16 * 7)
            dve.wait_ge(rel_ok, 1)
            nc.vector.nop().then_inc(acc_done, 1)

            def step(s, counts):
                for k in range(K):
                    g2_, g3, g5 = (Back(counts, k, lag) for lag in (2, 3, 5))
                    b = k % 2
                    norm1, norm2 = live(s, k, 2), live(s, k, 5)
                    if norm1 or norm2:
                        cols = slice(0 if norm1 else 1, 2 if norm2 else 1)
                        dve.wait_ge(std_ready[g2_.slot], g2_.count)
                        nc.vector.reciprocal(rstd[:, b, cols, :], std[:, b, cols, :]).then_inc(rstd_ready[g2_.slot], 1)
                    if k == 2 and live(s, k, 7):
                        base = dve.value_load(base_i[0:1, bass.ds(s - 2, 1)], min_val=0, max_val=N - 1)
                        dve.wait_ge(o_ready, counts[-2])
                        part = acc[:, bass.ds(base, SPAN)]
                        nc.vector.tensor_tensor(part, part, ps_o[:, 0:SPAN], ALU.add).then_inc(acc_done, 1)
                    if live(s, k, 0):
                        dve.wait_ge(dstbc_in[k // 2], counts[0] * 16)
                        nc.vector.tensor_scalar(pick[:, k % 2, :], dst_bc[:, k, :],
                                                win_node[:].rearrange("p s k -> p (s k)")[:, bass.ds(s * K + k, 1)],
                                                None, ALU.is_equal).then_inc(pick_ready[k], 1)
                    if norm2:
                        tiles = bass.ds(s * (K * T) + (k - 5) * T, T)
                        onehot = seg[:, g5.slot, :, :]
                        rel = dst_rel[:].rearrange("p s k t -> p (s k t)")[:, tiles]
                        nc.vector.tensor_tensor(onehot, iota_row[:].unsqueeze(1).to_broadcast([P, T, W]),
                                                rel.unsqueeze(2).to_broadcast([P, T, W]),
                                                ALU.is_equal).then_inc(onehot_ready[g5.slot], 1)
                        dve.wait_ge(rstd_ready[g2_.slot], g2_.count)
                        dve_scale2(ps_h[g5.buf], rstd[:, b, 1, :]).then_inc(t2_ready[g5.slot], 1)
                    if live(s, k, 3):
                        dve.wait_ge(aff_ready[g3.slot], g3.count)
                        dve_leaky1(g3.buf).then_inc(z_ready[g3.slot], 1)
                    if norm2:
                        dve.wait_ge(t2_ready[g5.slot], g5.count)
                        dve_shift2().then_inc(u2_ready[g5.slot], 1)
                        dve.wait_ge(onehot_ready[g5.slot], g5.count)
                        nc.vector.tensor_tensor(onehot, onehot,
                                                ew_all[:, tiles].unsqueeze(2).to_broadcast([P, T, W]), ALU.mult)
                        dve.wait_ge(u2_ready[g5.slot], g5.count)
                        dve_leaky2(g5.slot).then_inc(y_ready[g5.slot], 1)

            def fast():
                supersteps(dve, step)
                dve.wait_ge(acc_done, S + 1)
                nc.vector.nop().then_inc(sums_done, 1)

            def general():
                nc.vector.nop().then_inc(gen["acc"], 1)
                with dve.Fori(0, G) as g:
                    n = dve.snap(g + 1)
                    dve.wait_ge(gen["std1"], n)
                    nc.vector.reciprocal(rstd[:, 0, 0, :], std[:, 0, 0, :]).then_inc(gen["rstd1"], 1)
                    dve.wait_ge(gen["aff"], n)
                    dve_leaky1(0).then_inc(gen["z"], 1)
                    dve.wait_ge(gen["std2"], n)
                    nc.vector.reciprocal(rstd[:, 0, 1, :], std[:, 0, 1, :]).then_inc(gen["rstd2"], 1)
                    dve.wait_ge(gen["rstd2"], n)
                    dve_scale2(ps_h[0], rstd[:, 0, 1, :]).then_inc(gen["t2"], 1)
                    dve.wait_ge(gen["t2"], n)
                    dve_shift2().then_inc(gen["u2"], 1)
                    dve.wait_ge(gen["u2"], n)
                    dve_leaky2(0).then_inc(gen["y"], 1)
                    dve.wait_ge(gen["y"], n)
                    for t in range(T):
                        weighted = y[:, 0, t, :]
                        ins = nc.vector.tensor_scalar(weighted, weighted, ew_all[:, bass.ds(g * T + t, 1)], None, ALU.mult)
                    with dve.Fori(0, NW) as w:
                        m = dve.snap(g * NW + w + 1)
                        for t in range(T):
                            ins = nc.vector.tensor_scalar(seg_wide[:, t, :], iota_wide[:], wide_off[:, bass.ds(w, 1)],
                                                          dst_f[:, bass.ds(g * T + t, 1)], ALU.add, ALU.is_equal)
                        ins.then_inc(gen["seg"], 1)
                        dve.wait_ge(gen["o"], m)
                        part = acc[:, bass.ds(w * WIDE + MARGIN, WIDE)]
                        nc.vector.tensor_tensor(part, part, ps_o[:], ALU.add).then_inc(gen["acc"], 1)
                        dve.wait_ge(gen["acc"], dve.snap(m + 1))
                nc.vector.nop().then_inc(sums_done, 1)

            both_paths(dve, fast, general)

            for n in range(NQ + 1):
                o = n - 1
                qo = o % 2
                if n < NQ:
                    m = batch(n)
                    q = n % 2
                    dve.wait_ge(fT_ready, n + 1)
                    for j in range(m):
                        ins = nc.vector.bn_stats(stf[:, q, j, :], last_banks[n % 4][:, j, :])
                    ins.then_inc(stf_ready, 1)
                if n >= 1:
                    mo = batch(o)
                    dve.wait_ge(stdf_ready, n)
                    if o >= 2:
                        dve.wait_ge(fin_ready, o - 1)
                    nc.vector.reciprocal(rstdf[:, qo, 0:mo], stdf[:, qo, 0:mo]).then_inc(rstdf_ready, 1)
                if n < NQ:
                    dve.wait_ge(stf_ready, n + 1)
                    for j in range(m):
                        ins = nc.vector.bn_aggr(mvf[:, q, j, :], stf[:, q, j, :])
                    ins.then_inc(mvf_ready, 1)
                if n >= 1:
                    dve.wait_ge(rstdf_ready, n)
                    nc.vector.scalar_tensor_tensor(nbias[:, qo, 0:mo], mvf[:, qo, 0:mo, 0], -1.0, rstdf[:, qo, 0:mo],
                                                   op0=ALU.mult, op1=ALU.mult).then_inc(nbias_ready, 1)


_INS = ["x", "src", "dst", "edge_weight", "L0_gnn_w1", "L0_gnn_b1", "L0_gnn_g1", "L0_gnn_be1",
        "L0_gnn_w2", "L0_gnn_b2", "L0_gnn_g2", "L0_gnn_be2"]


def kernel(**inputs):
    import numpy as _np
    import concourse.bacc as _bacc
    from concourse.bass_utils import run_bass_kernel_spmd as _run

    nc = _bacc.Bacc("TRN2", target_bir_lowering=False, num_devices=1)
    arrays, args = {}, []
    for name in _INS:
        a = _np.ascontiguousarray(inputs[name])
        arrays[f"in_{name}"] = a
        args.append(nc.dram_tensor(f"in_{name}", a.shape, mybir.dt.from_np(a.dtype), kind="ExternalInput").ap())
    shape = inputs["x"].shape
    args.append(nc.dram_tensor("out_0", shape, F32, kind="ExternalOutput").ap())
    gnn_layer(nc, *args)
    r = _run(nc, [arrays], core_ids=[0])
    return r.results[0]["out_0"]
```

```python
from contextlib import ExitStack

import concourse.bass as bass
from concourse import mybir

F32 = mybir.dt.float32
BF16 = mybir.dt.bfloat16
I32 = mybir.dt.int32
I16 = mybir.dt.int16
ALU = mybir.AluOpType
ACT = mybir.ActivationFunctionType
AX = mybir.AxisListType

P = 128
C = 128
T = 4
GE = T * P
J = 4
K = 8
W = 64
HOP = 32
MARGIN = 16
SPAN = HOP * (J - 1) + W
WIDE = 512
EPS = 1e-5
SLOPE = 0.2


def gnn_layer(nc, x, src, dst, ew, w1, b1, g1, be1, w2, b2, g2, be2, out):
    N = x.shape[0]
    E = src.shape[0]
    SE = J * GE
    S = (E + SE - 1) // SE
    G = S * J
    R = G // K
    NT = G * T
    IB = 7
    BT = NT // IB
    HB = ((0, 4), (4, IB))
    NN = (N + P - 1) // P
    NL = N - (NN - 1) * P
    NQ = (NN + 3) // 4
    NB = 4
    ACT_BATCHES = (5, 6, 7, 8)
    XL = [0, 4, 12, 24, 36, NN]
    ROWS = (MARGIN + N + SPAN + P - 1) // P * P
    NW = (N + WIDE - 1) // WIDE
    FT = E // P
    RE = E - FT * P
    rest_e = E % SE
    own_e = rest_e - (J - 1) * GE
    dst_pieces = 1 if rest_e == 0 else 2 + -(-(SE - rest_e) // own_e)
    assert BT * IB == NT and BT <= P and S <= P and G % 2 == 0
    assert rest_e == 0 or own_e > 0
    assert G > K
    assert RE > 0 and (IB - 1) * BT < FT < NT

    ctx = ExitStack()
    with ctx:
        def sb(name, shape, dt):
            return ctx.enter_context(nc.sbuf_tensor(name, shape, dt))

        def psum(name, shape, dt=F32):
            return ctx.enter_context(nc.psum_tensor(name, shape, dt))

        def sem(name):
            return ctx.enter_context(nc.semaphore(name))

        def sems(name, n=J):
            return [sem(f"{name}{k}") for k in range(n)]

        src_table = nc.dram_tensor("src_table", (NN * P, C), F32, kind="Internal").ap()
        dst_table = nc.dram_tensor("dst_table", (ROWS, 3 * C), BF16, kind="Internal").ap()
        dst16_dram = nc.dram_tensor("dst16_dram", (NT * P,), I16, kind="Internal").ap()

        W1S, W1D, W2, B1, B2 = range(5)
        raw = sb("raw", [P, 5, C], F32)
        mid = sb("mid", [P, 5, C], F32)
        raw_st = sb("raw_st", [P, 5, 6], F32)
        raw_mv = sb("raw_mv", [P, 5, 2], F32)
        b_part = sb("b_part", [P, 2, 3, C], BF16)
        b_rest = sb("b_rest", [P, 2, C], F32)
        b1_rows = sb("b1_rows", [P, 4, C], BF16)
        b2_rows = sb("b2_rows", [P, 4, C], BF16)
        g2_bc = sb("g2_bc", [P, C], F32)
        be2_bc = sb("be2_bc", [P, T, C], F32)
        g1_col = sb("g1_col", [P, 1], F32)
        be1_col = sb("be1_col", [P, 1], F32)
        eps_col = sb("eps_col", [P, 1], F32)
        ones_bf = sb("ones_bf", [P, P], BF16)
        ones_f = sb("ones_f", [P, P], F32)
        ident = sb("ident", [P, P], F32)
        ident_bf = sb("ident_bf", [P, P], BF16)
        less_mean = sb("less_mean", [P, P], F32)
        iota_row = sb("iota_row", [P, W], F32)
        iota_col = sb("iota_col", [W, 1], F32)
        iota_wide = sb("iota_wide", [P, WIDE], F32)
        wide_off = sb("wide_off", [P, NW], F32)
        win_off = sb("win_off", [P, J], F32)
        zero_bf = sb("zero_bf", [P, 3 * C], BF16)

        src_t = sb("src_t", [BT, IB, P], I32)
        dst_t = sb("dst_t", [BT, IB, P], I32)
        ew_t = sb("ew_t", [BT, IB, P], F32)
        src_tf = sb("src_tf", [BT, IB, P], F32)
        dst_tf = sb("dst_tf", [BT, IB, P], F32)
        dst16_t = sb("dst16_t", [BT, IB, P], I16)
        src_idx = sb("src_idx", [P, NT + 2 * T], I32)
        dst_idx = sb("dst_idx", [P, NT + 2 * T], I32)
        dst_f = sb("dst_f", [P, NT], F32)
        ew_all = sb("ew_all", [P, NT], F32)
        dst_rel = sb("dst_rel", [P, S, J, T], F32)
        dst_s = sb("dst_s", [S, J, GE], I32)
        dst_min = sb("dst_min", [S, J], F32)
        dst_max = sb("dst_max", [S, J], F32)
        miss = sb("miss", [S, 2, J], F32)
        base_col = sb("base_col", [S, 1], F32)
        base_diag = sb("base_diag", [S, S + 1], F32)
        base_bc = sb("base_bc", [P, S], F32)
        base_i = sb("base_i", [1, S + 1], I32)
        win_node = sb("win_node", [W, S, J], F32)

        x_all = sb("x_all", [P, NN, C], F32)
        tab_src = sb("tab_src", [P, NB, 4, C], F32)
        tab_dst = sb("tab_dst", [P, NB, 4, 3, C], BF16)
        tab_rest = sb("tab_rest", [P, 2, 4, C], F32)
        ACOLS = max(ROWS, MARGIN + NW * WIDE)
        acc = sb("acc", [P, ACOLS], F32)

        idx_slot = sb("idx_slot", [P, K // 2, 2 * T], I32)
        a_src = sb("a_src", [P, K, T, C], F32)
        dst_bc = sb("dst_bc", [W, K, GE], I16)
        pick = sb("pick", [W, 2, GE], BF16)
        win = sb("win", [W, K, 3, C], BF16)
        junk = sb("junk", [P, 2, 2, T, C], BF16)
        ssq = sb("ssq", [P, 2, 2, T], F32)
        std = sb("std", [P, 2, 2, T], F32)
        rstd = sb("rstd", [P, 2, 2, T], F32)
        cn = sb("cn", [P, 2, T, C], F32)
        aff = sb("aff", [P, 2, GE], F32)
        z = sb("z", [P, 2, GE], F32)
        t2 = sb("t2", [P, T, C], F32)
        u2 = sb("u2", [P, T, C], F32)
        y = sb("y", [P, J, T, C], F32)
        seg = sb("seg", [P, J, T, W], F32)

        idx2_slot = sb("idx2_slot", [P, 2, T], I32)
        b_dst = sb("b_dst", [P, T, 3 * C], BF16)

        seg_wide = x_all[:, 4 * NB:4 * NB + 4 * T, :].rearrange("p (t n) c -> p t (n c)", n=4)

        stf = sb("stf", [P, 2, 4, 6], F32)
        mvf = sb("mvf", [P, 2, 4, 2], F32)
        stdf = sb("stdf", [P, 2, 4], F32)
        rstdf = sb("rstdf", [P, 2, 4], F32)
        fin = x_all[:, 0:4 * NB, :].rearrange("p (b t) c -> p b t c", t=4)

        ps_c = [psum(f"ps_c{b}", [P, T, C]) for b in range(2)]
        ps_cT = psum("ps_cT", [P, GE])
        ps_h = [psum(f"ps_h{b}", [P, T, C]) for b in range(2)]
        ps_o = psum("ps_o", [P, 512])
        ps_t = [psum(f"ps_t{b}", [P, 512]) for b in range(2)]

        wide_banks = ps_c + ps_h

        w1_in = sem("w1_in")
        w_in = sem("w_in")
        v_in = sem("v_in")
        src_in = sem("src_in")
        dst_in = sem("dst_in")
        ew_in = sem("ew_in")
        dsts_in = sem("dsts_in")
        x_in = sems("x_in", len(XL) - 1)
        x_tail_in = sem("x_tail_in")
        zero_ok = sem("zero_ok")
        ident_ok = sem("ident_ok")
        const_ok = sem("const_ok")
        dve_own = sem("dve_own")
        centred = sem("centred")
        b_split = sem("b_split")
        src_cast = sem("src_cast")
        dst_cast = sem("dst_cast")
        dst16_cast = sem("dst16_cast")
        turned = sem("turned")
        turn_out = sem("turn_out")
        base_set = sem("base_set")
        base_ps = sem("base_ps")
        base_ok = sem("base_ok")
        rel_ok = sem("rel_ok")
        dst_rows = sem("dst_rows")
        dst16_out = sem("dst16_out")
        zero_out = sem("zero_out")
        node_T = sem("node_T")
        node_Tc = sem("node_Tc")
        node_A = sem("node_A")
        node_Ac = sems("node_Ac", 4)
        node_B = sem("node_B")
        node_hi = sem("node_hi")
        node_r1 = sem("node_r1")
        node_mid = sem("node_mid")
        node_lo = sem("node_lo")
        src_out = sems("src_out", NB)
        tab_out = sems("tab_out", NB)

        idx_in = sems("idx_in", K // 2)
        gathered = sems("gathered", K)
        gathers_begun = sem("gathers_begun")
        dstbc_in = sems("dstbc_in", K // 2)
        win_in = sems("win_in", K // 2)
        pick_ready = sems("pick_ready")
        c_ready = sems("c_ready")
        ssq1_ready = sems("ssq1_ready")
        std_ready = sems("std_ready")
        rstd_ready = sems("rstd_ready")
        cn_ready = sems("cn_ready")
        cT_ready = sems("cT_ready")
        aff_ready = sems("aff_ready")
        z_ready = sems("z_ready")
        h_ready = sems("h_ready")
        ssq2_ready = sems("ssq2_ready")
        t2_ready = sems("t2_ready")
        u2_ready = sems("u2_ready")
        y_ready = sems("y_ready")
        onehot_ready = sems("onehot_ready")
        o_ready = sem("o_ready")
        acc_done = sem("acc_done")

        gen_idx = sems("gen_idx", 2)
        gen_gathered = gathered[0:2]
        gen = {"c": c_ready[0], "ssq1": ssq1_ready[0], "std1": std_ready[0], "rstd1": rstd_ready[0],
               "cn": cn_ready[0], "cT": cT_ready[0], "aff": aff_ready[0], "z": z_ready[0], "h": h_ready[0],
               "ssq2": ssq2_ready[0], "std2": std_ready[1], "rstd2": rstd_ready[1], "t2": t2_ready[0],
               "u2": u2_ready[0], "y": y_ready[0], "seg": onehot_ready[0], "o": o_ready, "acc": acc_done}

        sums_done = sem("sums_done")
        fT_ready = sem("fT_ready")
        stf_ready = sem("stf_ready")
        mvf_ready = sem("mvf_ready")
        stdf_ready = sem("stdf_ready")
        rstdf_ready = sem("rstdf_ready")
        fin_ready = sem("fin_ready")
        out_done = sems("out_done", NB)

        block = ctx.enter_context(nc.Block())

        def live(r, k, lag):
            return 0 <= K * r + k - lag < G if isinstance(r, int) else True

        class Back:

            def __init__(self, counts, turns, k, lag):
                self.slot = (k - lag) % K
                self.place = self.slot % J
                self.buf = self.slot % 2
                self.count = counts[(k - lag) // J]
                self.turn = turns[(k - lag) // K]

        LAST = (G + 6) // K

        def rounds(eng, step):
            B = K // J
            ahead = range(-B, B)
            step(0, {q: q + 1 for q in ahead}, {0: 1, -1: 0})
            with eng.Fori(1, R) as r:
                step(r, {q: eng.snap(r * B + (q + 1)) for q in ahead}, {0: eng.snap(r + 1), -1: r})
            for r in range(R, LAST + 1):
                step(r, {q: r * B + q + 1 for q in ahead}, {0: r + 1, -1: r})

        def batch(n):
            return min(4, NN - 4 * n)

        def both_paths(eng, fast, general):
            eng.wait_ge(base_ok, 1)
            misses = eng.value_load(base_i[0:1, S:S + 1], min_val=0, max_val=2 * G)
            with eng.If(misses == 0):
                fast()
            with eng.Else():
                general()

        def act_sum_squares(which, junk_buf, bank, sums):
            for t in range(T):
                ins = nc.scalar.activation(junk[:, which, junk_buf, t, :], bank[:, t, :], ACT.Square,
                                           accum_out=sums[:, t:t + 1])
            return ins

        def act_std(b, a, z_):
            return nc.scalar.activation(std[:, b, a:z_, :], ssq[:, b, a:z_, :], ACT.Sqrt, bias=eps_col[:, 0:1],
                                        scale=1.0 / C)

        def act_normalise(b, bank, rstds):
            for t in range(T):
                ins = nc.scalar.activation(cn[:, b, t, :], bank[:, t, :], ACT.Copy, scale=rstds[:, t:t + 1])
            return ins

        def act_affine(b):
            return nc.scalar.activation(aff[:, b, :], ps_cT[:], ACT.Identity, bias=be1_col[:, 0:1],
                                        scale=g1_col[:, 0:1])

        def pe_source_rows(bank, slot):
            nc.tensor.matmul(bank[:], ident[:], a_src[:, slot, :, :], start=True, stop=True)

        def pe_turn(b):
            for t in range(T):
                mm = nc.tensor.transpose(ps_cT[:, t * P:(t + 1) * P], cn[:, b, t, :], ident[:])
            return mm

        def pe_second_product(b, bank):
            nc.tensor.matmul(bank[:], ones_bf[:], b2_rows[:], start=True, stop=True)
            for t in range(T):
                mm = nc.tensor.matmul(bank[:, t, :], z[:, b, t * P:(t + 1) * P], mid[:, W2, :],
                                      start=False, stop=True, skip_group_check=True)
            return mm

        def dve_leaky1(b):
            return nc.vector.scalar_tensor_tensor(z[:, b, :], aff[:, b, :], SLOPE, aff[:, b, :],
                                                  op0=ALU.mult, op1=ALU.max)

        def dve_scale2(bank, rstds):
            for t in range(T):
                ins = nc.vector.scalar_tensor_tensor(t2[:, t, :], bank[:, t, :], rstds[:, t:t + 1], g2_bc[:],
                                                     op0=ALU.mult, op1=ALU.mult)
            return ins

        def dve_shift2():
            return nc.vector.tensor_tensor(u2[:], t2[:], be2_bc[:], ALU.add)

        def dve_leaky2(slot):
            return nc.vector.scalar_tensor_tensor(y[:, slot, :, :], u2[:], SLOPE, u2[:], op0=ALU.mult, op1=ALU.max)

        def outs(n, q):
            total = 0
            for i in range(q, n, NB):
                m = batch(i)
                full = m if 4 * i + m < NN or NL == P else m - 1
                total += (full > 0) + (full < m)
            return total

        def uses(q):
            return (NQ - q + NB - 1) // NB

        @block.sync
        def _(sp):
            sp.dma_start(raw[:, W1S:W1D + 1, :], w1.rearrange("(h p) c -> p h c", p=P)).then_inc(w1_in, 16)
            for i, (a, b) in enumerate(zip(XL[:-1], XL[1:])):
                b = min(b, NN - 1)
                sp.dma_start(x_all[:, a:b, :], x[a * P:b * P].rearrange("(n p) c -> p n c", p=P)).then_inc(x_in[i], 16)
            sp.wait_ge(zero_ok, 1)
            sp.dma_start(x_all[0:NL, NN - 1, :], x[(NN - 1) * P:N]).then_inc(x_tail_in, 16)
            for dest, dram, done in ((src_t, src, src_in), (dst_t, dst, dst_in), (ew_t, ew, ew_in)):
                full = (IB - 1) * BT
                sp.dma_start(dest[:, 0:IB - 1, :],
                             dram[0:full * P].rearrange("(b p e) -> p b e", b=IB - 1, e=P)).then_inc(done, 16)
                sp.dma_start(dest[0:FT - full, IB - 1, :],
                             dram[full * P:FT * P].rearrange("(p e) -> p e", e=P)).then_inc(done, 16)
                sp.dma_start(dest[FT - full:FT - full + 1, IB - 1, 0:RE],
                             dram[FT * P:E].rearrange("(p e) -> p e", p=1)).then_inc(done, 16)
            outside = []
            for r0, r1 in ((0, MARGIN), (MARGIN + NN * P, ROWS)):
                outside += [(r, min(r + P, r1)) for r in range(r0, r1, P)]
            zeros = len(outside)
            for n in range(NQ):
                m = batch(n)
                if n == 3:
                    sp.dma_start(g1_col[:], g1.rearrange("(p o) -> p o", o=1)).then_inc(v_in, 16)
                    sp.dma_start(be1_col[:], be1.rearrange("(p o) -> p o", o=1)).then_inc(v_in, 16)
                    sp.dma_start(g2_bc[:], g2.partition_broadcast(P)).then_inc(v_in, 16)
                if 4 <= n < 4 + T:
                    sp.dma_start(be2_bc[:, n - 4, :], be2.partition_broadcast(P)).then_inc(v_in, 16)
                if n == 9:
                    sp.wait_ge(const_ok, 1)
                    for r0, r1 in outside:
                        sp.dma_start(dst_table[r0:r1], zero_bf[0:r1 - r0]).then_inc(zero_out, 16)
                sp.wait_ge(node_Ac[n % 4], n // 4 + 1)
                sp.dma_start(src_table[4 * n * P:(4 * n + m) * P].rearrange("(t p) c -> p t c", p=P),
                             tab_src[:, n % NB, 0:m, :]).then_inc(src_out[n % NB], 16)
            sp.wait_ge(turn_out, 2)
            for h in range(K // 2):
                sp.dma_start(idx_slot[:, h, :], src_idx[:, 2 * T * h:2 * T * (h + 1)]).then_inc(idx_in[h], 16)
            sp.wait_ge(dst16_cast, 1)
            sp.dma_start(dst16_dram.rearrange("(b p e) -> p b e", b=IB, e=P), dst16_t[:]).then_inc(dst16_out, 16)
            for n in range(NQ):
                m = batch(n)
                sp.wait_ge(node_lo, n + 1)
                r0 = MARGIN + 4 * n * P
                sp.dma_start(dst_table[r0:r0 + m * P].rearrange("(t p) c -> p t c", p=P),
                             tab_dst[:, n % NB, 0:m, :, :].rearrange("p t q c -> p t (q c)")).then_inc(
                                 tab_out[n % NB], 16)
            sp.wait_ge(dst16_out, 16)

            def table_stored():
                sp.wait_ge(zero_out, 16 * zeros)
                for q in range(NB):
                    sp.wait_ge(tab_out[q], 16 * uses(q))

            def step(r, counts, turns):
                for h in range(K // 2):
                    k0 = 2 * h
                    if not live(r, k0, 0):
                        return
                    if k0 % J == 0:
                        base = sp.value_load(base_i[0:1, bass.ds(r * (K // J) + k0 // J, 1)], min_val=0, max_val=N - 1)
                    later = not isinstance(r, int) or r > 0
                    if later:
                        sp.wait_ge(gathered[k0], turns[-1] * (16 * T))
                        sp.wait_ge(gathered[k0 + 1], turns[-1] * (16 * T))
                        sp.dma_start(idx_slot[:, h, :],
                                     src_idx[:, bass.ds(r * (K * T) + k0 * T, 2 * T)]).then_inc(idx_in[h], 16)
                        sp.wait_ge(pick_ready[(k0 + 1) % J], counts[k0 // J - K // J])
                    sp.dma_start(dst_bc[:, k0:k0 + 2, :].rearrange("p k e -> p (k e)"),
                                 dst16_dram[bass.ds(r * (K * GE) + k0 * GE, 2 * GE)].partition_broadcast(W)
                                 ).then_inc(dstbc_in[h], 16)
                    if later:
                        sp.wait_ge(c_ready[(k0 + 1) % J], counts[k0 // J - K // J])
                    elif h == 0:
                        table_stored()
                    for k in (k0, k0 + 1):
                        sp.dma_start(win[:, k, :, :].rearrange("w q c -> w (q c)"),
                                     dst_table[bass.ds(base + HOP * (k % J), W), :]).then_inc(win_in[h], 16)

            def general():
                table_stored()

            both_paths(sp, lambda: rounds(sp, step), general)

            for n in range(NQ):
                m = batch(n)
                full = m if 4 * n + m < NN or NL == P else m - 1
                sp.wait_ge(fin_ready, n + 1)
                if full:
                    sp.dma_start(out[4 * n * P:(4 * n + full) * P].rearrange("(t p) c -> p t c", p=P),
                                 fin[:, n % NB, 0:full, :]).then_inc(out_done[n % NB], 16)
                if full < m:
                    sp.dma_start(out[(NN - 1) * P:N], fin[0:NL, n % NB, full, :]).then_inc(out_done[n % NB], 16)
            for q in range(NB):
                sp.wait_ge(out_done[q], 16 * outs(NQ, q))

        @block.gpsimd
        def _(pool):
            nc.gpsimd.memset(ident[:], 0.0).then_inc(ident_ok, 1)
            nc.gpsimd.memset(eps_col[:], EPS)
            nc.gpsimd.memset(x_all[:, NN - 1, :], 0.0)
            nc.gpsimd.memset(src_t[:, IB - 1, :], 0)
            nc.gpsimd.memset(dst_t[:, IB - 1, :], 0)
            nc.gpsimd.memset(ew_t[:, IB - 1, :], 0.0).then_inc(zero_ok, 1)
            pool.dma_start(raw[:, B1, :], b1.partition_broadcast(P)).then_inc(w_in, 16)
            pool.dma_start(raw[:, W2, :], w2).then_inc(w_in, 16)
            pool.dma_start(raw[:, B2, :], b2.partition_broadcast(P)).then_inc(w_in, 16)
            pool.wait_ge(ident_ok, 1)
            nc.gpsimd.affine_select(out=ident[:], in_=ident[:], compare_op=ALU.not_equal, fill=1.0, base=0,
                                    pattern=[[-1, P]], channel_multiplier=1).then_inc(ident_ok, 1)
            nc.gpsimd.memset(ones_f[:], 1.0)
            nc.gpsimd.memset(ones_bf[:], 1.0)
            nc.gpsimd.memset(b1_rows[:], 0.0)
            nc.gpsimd.memset(b2_rows[:], 0.0)
            nc.gpsimd.memset(zero_bf[:], 0.0)
            nc.gpsimd.memset(src_idx[:, NT:NT + 2 * T], 0)
            nc.gpsimd.memset(dst_idx[:, NT:NT + 2 * T], 0)
            nc.gpsimd.memset(acc[:, 0:MARGIN], 0.0)
            nc.gpsimd.memset(acc[:, MARGIN + NN * P:ACOLS], 0.0)
            nc.gpsimd.iota(iota_row[:], [[1, W]], base=0, channel_multiplier=0,
                           allow_small_or_imprecise_dtypes=True)
            nc.gpsimd.iota(iota_wide[:], [[1, WIDE]], base=0, channel_multiplier=0,
                           allow_small_or_imprecise_dtypes=True)
            nc.gpsimd.iota(wide_off[:], [[WIDE, NW]], base=0, channel_multiplier=0,
                           allow_small_or_imprecise_dtypes=True)
            nc.gpsimd.iota(win_off[:], [[HOP, J]], base=-MARGIN, channel_multiplier=0,
                           allow_small_or_imprecise_dtypes=True)
            nc.gpsimd.iota(iota_col[:], [[0, 1]], base=0, channel_multiplier=1,
                           allow_small_or_imprecise_dtypes=True).then_inc(const_ok, 1)
            for q in range(NB):
                pool.wait_ge(src_out[q], 16 * uses(q))

            def gather(dest, table, index, done):
                nc.gpsimd.indirect_dma_start(out=dest, out_offset=None, in_=table,
                                             in_offset=bass.IndirectOffsetOnAxis(ap=index, axis=0)).then_inc(done, 16)

            def step(r, counts, turns):
                for k in range(K):
                    if not live(r, k, 0):
                        return
                    if k % 2 == 0:
                        pool.wait_ge(idx_in[k // 2], turns[0] * 16)
                    if not isinstance(r, int) or r > 0:
                        pool.wait_ge(c_ready[k % J], counts[k // J - K // J])
                    pool.sem_inc(gathers_begun, 1)
                    for t in range(T):
                        gather(a_src[:, k, t, :], src_table, idx_slot[:, k // 2, (k % 2) * T + t:(k % 2) * T + t + 1],
                               gathered[k])

            def general():
                pool.wait_ge(dst_rows, 1)
                for q in range(NB):
                    pool.wait_ge(tab_out[q], 16 * uses(q))
                for h in range(K // 2):
                    pool.wait_ge(idx_in[h], 16)
                nc.gpsimd.tensor_copy(idx_slot[:, 0, 0:T], src_idx[:, 0:T])
                nc.gpsimd.tensor_copy(idx2_slot[:, 0, :], dst_idx[:, 0:T]).then_inc(gen_idx[0], 1)
                with pool.Fori(0, G // 2) as i:
                    n = pool.snap(i + 1)
                    for b in range(2):
                        before = pool.snap(i * (2 * NW) + (b * NW + 1))
                        pool.wait_ge(gen_idx[b], n)
                        pool.wait_ge(gen["acc"], before)
                        at = i * (2 * T) + (b + 1) * T
                        nc.gpsimd.tensor_copy(idx_slot[:, 1 - b, 0:T], src_idx[:, bass.ds(at, T)])
                        nc.gpsimd.tensor_copy(idx2_slot[:, 1 - b, :],
                                              dst_idx[:, bass.ds(at, T)]).then_inc(gen_idx[1 - b], 1)
                        for t in range(T):
                            gather(a_src[:, 0, t, :], src_table, idx_slot[:, b, t:t + 1], gen_gathered[b])
                            gather(b_dst[:, t, :], dst_table, idx2_slot[:, b, t:t + 1], gen_gathered[b])

            both_paths(pool, lambda: rounds(pool, step), general)

        @block.scalar
        def _(act):
            act.wait_ge(zero_ok, 1)
            nc.scalar.activation(std[:, 0, 0, 0:1], eps_col[:, 0:1], ACT.Sqrt)
            full = E // SE
            act.dma_start(dst_s[0:full],
                          dst[0:full * SE].rearrange("(s k e) -> s k e", k=J, e=GE)).then_inc(dsts_in, 16)
            if rest_e:
                row = dst_s[full:full + 1].rearrange("s k e -> s (k e)")
                act.dma_start(row[:, 0:rest_e], dst[full * SE:E].rearrange("(s e) -> s e", s=1)).then_inc(dsts_in, 16)
                at = rest_e
                while at < SE:
                    n = min(own_e, SE - at)
                    act.dma_start(row[:, at:at + n], dst[E - n:E].rearrange("(s e) -> s e", s=1)).then_inc(dsts_in, 16)
                    at += n

            def evacuate(q, dest):
                for half, (b0, b1_) in enumerate(HB):
                    act.wait_ge(turned, 2 * q + half + 1)
                    nc.scalar.copy(dest[:, b0 * BT:b1_ * BT],
                                   (ps_cT, ps_o)[half][:, 0:(b1_ - b0) * BT]).then_inc(turn_out, 1)

            for n in range(NQ):
                m = batch(n)
                act.wait_ge(node_T, n + 1)
                at = MARGIN + 4 * n * P
                nc.scalar.copy(acc[:, at:at + m * P], ps_t[n % 2][:, 0:m * P]).then_inc(node_Tc, 1)
                if n - 1 in ACT_BATCHES:
                    o = n - 1
                    act.wait_ge(node_A, o + 1)
                    if o >= NB:
                        act.wait_ge(src_out[o % NB], 16 * (o // NB))
                    nc.scalar.copy(tab_src[:, o % NB, 0:batch(o), :],
                                   wide_banks[o % 4][:, 0:batch(o), :]).then_inc(node_Ac[o % 4], 1)
                if n == 6:
                    act.wait_ge(src_in, 48)
                    nc.scalar.copy(src_tf[:], src_t[:]).then_inc(src_cast, 1)
                if n == 8:
                    act.wait_ge(dst_in, 48)
                    nc.scalar.copy(dst16_t[:], dst_t[:]).then_inc(dst16_cast, 1)
                if n == 10:
                    nc.scalar.copy(dst_tf[:], dst_t[:]).then_inc(dst_cast, 1)
                if n == 11:
                    evacuate(0, src_idx)

            for n in range(NQ + 1):
                if n < NQ:
                    m = batch(n)
                    act.wait_ge(node_B, n + 1)
                    if n >= NB:
                        act.wait_ge(tab_out[n % NB], 16 * (n // NB))
                    nc.scalar.copy(tab_dst[:, n % NB, 0:m, 0, :],
                                   wide_banks[(NQ + n) % 4][:, 0:m, :]).then_inc(node_hi, 1)
                if n >= 1:
                    o = n - 1
                    m = batch(o)
                    act.wait_ge(node_r1, o + 1)
                    nc.scalar.copy(tab_dst[:, o % NB, 0:m, 1, :], tab_rest[:, o % 2, 0:m, :]).then_inc(node_mid, 1)
                if n == 3:
                    evacuate(1, dst_f)
                if n == 6:
                    evacuate(2, ew_all)
            act.wait_ge(v_in, 16 * 7)

            def step(r, counts, turns):
                for k in range(K):
                    b = k % 2
                    g2_, g3, g5 = (Back(counts, turns, k, lag) for lag in (2, 3, 5))
                    norm1, norm2 = live(r, k, 2), live(r, k, 5)
                    if norm2:
                        act.wait_ge(h_ready[g5.place], g5.count)
                        act_sum_squares(1, g5.buf, ps_h[g5.buf], ssq[:, b, 1, :]).then_inc(ssq2_ready[g5.place], 1)
                    if norm1 or norm2:
                        if norm1:
                            act.wait_ge(ssq1_ready[g2_.place], g2_.count)
                        if norm2:
                            act.wait_ge(ssq2_ready[g5.place], g5.count)
                        act_std(b, 0 if norm1 else 1, 2 if norm2 else 1).then_inc(std_ready[g2_.place], 1)
                    if live(r, k, 3):
                        act.wait_ge(cT_ready[g3.place], g3.count)
                        act_affine(g3.buf).then_inc(aff_ready[g3.place], 1)
                    if norm1:
                        act.wait_ge(rstd_ready[g2_.place], g2_.count)
                        act_normalise(g2_.buf, ps_c[g2_.buf], rstd[:, b, 0, :]).then_inc(cn_ready[g2_.place], 1)
                    if live(r, k, 1):
                        g = Back(counts, turns, k, 1)
                        act.wait_ge(c_ready[g.place], g.count)
                        act_sum_squares(0, g.buf, ps_c[g.buf], ssq[:, 1 - b, 0, :]).then_inc(ssq1_ready[g.place], 1)

            def general():
                with act.Fori(0, G) as g:
                    n = act.snap(g + 1)
                    act.wait_ge(gen["c"], n)
                    act_sum_squares(0, 0, ps_c[0], ssq[:, 0, 0, :]).then_inc(gen["ssq1"], 1)
                    act.wait_ge(gen["ssq1"], n)
                    act_std(0, 0, 1).then_inc(gen["std1"], 1)
                    act.wait_ge(gen["rstd1"], n)
                    act_normalise(0, ps_c[0], rstd[:, 0, 0, :]).then_inc(gen["cn"], 1)
                    act.wait_ge(gen["cT"], n)
                    act_affine(0).then_inc(gen["aff"], 1)
                    act.wait_ge(gen["h"], n)
                    act_sum_squares(1, 0, ps_h[0], ssq[:, 0, 1, :]).then_inc(gen["ssq2"], 1)
                    act.wait_ge(gen["ssq2"], n)
                    act_std(0, 1, 2).then_inc(gen["std2"], 1)

            both_paths(act, lambda: rounds(act, step), general)

            for n in range(NQ + 1):
                if n < NQ:
                    m = batch(n)
                    act.wait_ge(mvf_ready, n + 1)
                    nc.scalar.activation(stdf[:, n % 2, 0:m], mvf[:, n % 2, 0:m, 1], ACT.Sqrt,
                                         bias=eps_col[:, 0:1]).then_inc(stdf_ready, 1)
                if n >= 1:
                    o = n - 1
                    q = o % 2
                    m = batch(o)
                    act.wait_ge(rstdf_ready, n)
                    if o >= NB:
                        act.wait_ge(out_done[o % NB], 16 * outs(o, o % NB))
                    for j in range(m):
                        ins = nc.scalar.activation(fin[:, o % NB, j, :], wide_banks[o % 4][:, j, :], ACT.Copy,
                                                   scale=rstdf[:, q, j:j + 1])
                    ins.then_inc(fin_ready, 1)

        @block.tensor
        def _(pe):
            def turn_indices(q, tile_rows, cast, done):
                pe.wait_ge(cast, done)
                for half, (b0, b1_) in enumerate(HB):
                    if q:
                        pe.wait_ge(turn_out, 2 * (q - 1) + half + 1)
                    bank = (ps_cT, ps_o)[half]
                    for blk in range(b0, b1_):
                        at = (blk - b0) * BT
                        mm = nc.tensor.transpose(bank[:, at:at + BT], tile_rows[:, blk, :], ident[0:BT, 0:BT])
                    mm.then_inc(turned, 1)

            def node_turn(n):
                m = batch(n)
                for i, a in enumerate(XL[:-1]):
                    if 4 * n + m > a:
                        pe.wait_ge(x_in[i], 16)
                if n == NQ - 1:
                    pe.wait_ge(x_tail_in, 16)
                if n >= 2:
                    pe.wait_ge(node_Tc, n - 1)
                for j in range(m):
                    mm = nc.tensor.transpose(ps_t[n % 2][:, j * P:(j + 1) * P], x_all[:, 4 * n + j, :], ident[:])
                mm.then_inc(node_T, 1)

            def product(n, w, bank, start):
                for j in range(batch(n)):
                    at = MARGIN + (4 * n + j) * P
                    mm = nc.tensor.matmul(bank[:, j, :], acc[:, at:at + P], mid[:, w, :], start=start, stop=True,
                                          skip_group_check=True)
                return mm

            pe.wait_ge(ident_ok, 2)
            node_turn(0)
            node_turn(1)
            pe.wait_ge(centred, 1)
            for n in range(NQ):
                pe.wait_ge(node_Tc, n + 1)
                if n >= 4:
                    pe.wait_ge(node_Ac[n % 4], n // 4)
                product(n, W1S, wide_banks[n % 4], True).then_inc(node_A, 1)
                if n + 2 < NQ:
                    node_turn(n + 2)
                if n == 9:
                    turn_indices(0, src_tf, src_cast, 1)
                if n == NQ - 1:
                    pe.wait_ge(base_set, 1)
                    pe.wait_ge(turn_out, 2)
                    nc.tensor.matmul(ps_o[:, 0:S + 1], ones_f[0:S, :], base_diag[:], start=True,
                                     stop=True).then_inc(base_ps, 1)
            pe.wait_ge(b_split, 1)
            pe.wait_ge(base_ok, 1)
            for n in range(NQ):
                if n < 4:
                    o = NQ + n - 4
                    pe.wait_ge(node_Ac[o % 4], o // 4 + 1)
                else:
                    pe.wait_ge(node_r1, n - 3)
                bank = wide_banks[(NQ + n) % 4]
                nc.tensor.matmul(bank[:, 0:batch(n), :], ones_bf[:], b1_rows[:, 0:batch(n), :], start=True, stop=True)
                product(n, W1D, bank, False).then_inc(node_B, 1)
                if n == 1:
                    turn_indices(1, dst_tf, dst_cast, 1)
                if n == 4:
                    turn_indices(2, ew_t, ew_in, 48)
            pe.wait_ge(node_r1, NQ)
            pe.wait_ge(turn_out, 6)
            pe.wait_ge(rel_ok, 1)
            pe.wait_ge(b_split, 2)

            def step(r, counts, turns):
                for k in range(K):
                    if live(r, k, 3):
                        g = Back(counts, turns, k, 3)
                        pe.wait_ge(cn_ready[g.place], g.count)
                        if live(r, k, 4):
                            g4 = Back(counts, turns, k, 4)
                            pe.wait_ge(aff_ready[g4.place], g4.count)
                        pe_turn(g.buf).then_inc(cT_ready[g.place], 1)
                    if live(r, k, 4):
                        g = Back(counts, turns, k, 4)
                        if live(r, k, 6):
                            g6 = Back(counts, turns, k, 6)
                            pe.wait_ge(t2_ready[g6.place], g6.count)
                        pe.wait_ge(z_ready[g.place], g.count)
                        pe_second_product(g.buf, ps_h[g.buf]).then_inc(h_ready[g.place], 1)
                    if live(r, k, 1):
                        g = Back(counts, turns, k, 1)
                        if live(r, k, 3):
                            g3 = Back(counts, turns, k, 3)
                            pe.wait_ge(cn_ready[g3.place], g3.count)
                        pe.wait_ge(gathered[g.slot], g.turn * (16 * T))
                        pe_source_rows(ps_c[g.buf], g.slot)
                        pe.wait_ge(pick_ready[g.place], g.count)
                        pe.wait_ge(win_in[g.slot // 2], g.turn * 32)
                        for t in range(T):
                            for part in range(3):
                                mm = nc.tensor.matmul(ps_c[g.buf][:, t, :], pick[:, g.buf, t * P:(t + 1) * P],
                                                      win[:, g.slot, part, :], start=False, stop=True,
                                                      skip_group_check=True)
                        mm.then_inc(c_ready[g.place], 1)
                    if live(r, k, 6):
                        g = Back(counts, turns, k, 6)
                        pe.wait_ge(y_ready[g.place], g.count)
                        if g.place == 0:
                            pe.wait_ge(acc_done, g.count)
                        at = HOP * g.place
                        for t in range(T):
                            mm = nc.tensor.matmul(ps_o[:, at:at + W], y[:, g.place, t, :], seg[:, g.place, t, :],
                                                  start=(g.place == 0 and t == 0), stop=True, skip_group_check=True)
                        if g.place == J - 1:
                            mm.then_inc(o_ready, 1)

            def general():
                with pe.Fori(0, G // 2) as i:
                    for b in range(2):
                        n = pe.snap(2 * i + (b + 1))
                        pe.wait_ge(gen_gathered[b], (i + 1) * (16 * 2 * T))
                        pe_source_rows(ps_c[0], 0)
                        for part in range(3):
                            mm = nc.tensor.matmul(ps_c[0][:], ident_bf[:],
                                                  b_dst[:, :, part * C:(part + 1) * C], start=False,
                                                  stop=True, skip_group_check=True)
                        mm.then_inc(gen["c"], 1)
                        pe.wait_ge(gen["cn"], n)
                        pe_turn(0).then_inc(gen["cT"], 1)
                        pe.wait_ge(gen["z"], n)
                        pe_second_product(0, ps_h[0]).then_inc(gen["h"], 1)
                        with pe.Fori(0, NW) as w:
                            pe.wait_ge(gen["seg"], i * (2 * NW) + w + (b * NW + 1))
                            for t in range(T):
                                mm = nc.tensor.matmul(ps_o[:], y[:, 0, t, :], seg_wide[:, t, :],
                                                      start=(t == 0), stop=(t == T - 1))
                            mm.then_inc(gen["o"], 1)

            both_paths(pe, lambda: rounds(pe, step), general)

            pe.wait_ge(sums_done, 1)
            for n in range(NQ):
                m = batch(n)
                if n >= 4:
                    pe.wait_ge(fin_ready, n - 3)
                for j in range(m):
                    at = MARGIN + (4 * n + j) * P
                    mm = nc.tensor.matmul(wide_banks[n % 4][:, j, :], acc[:, at:at + P], less_mean[:], start=True,
                                          stop=True)
                mm.then_inc(fT_ready, 1)

        @block.vector
        def _(dve):
            own = [0]

            def then(ins):
                own[0] += 1
                ins.then_inc(dve_own, 1)
                dve.wait_ge(dve_own, own[0])

            def centre(rows, arrived, count):
                dve.wait_ge(arrived, count)
                for i in rows:
                    ins = nc.vector.bn_stats(raw_st[:, i, :], raw[:, i, :])
                then(ins)
                for i in rows:
                    ins = nc.vector.bn_aggr(raw_mv[:, i, :], raw_st[:, i, :])
                then(ins)
                for i in rows:
                    ins = nc.vector.tensor_scalar(mid[:, i, :], raw[:, i, :], raw_mv[:, i, 0:1], None, ALU.subtract)
                ins.then_inc(centred, 1)

            def split_bias(i, b_bc, rows):
                then(nc.vector.tensor_copy(b_part[:, i, 0, :], b_bc))
                then(nc.vector.tensor_tensor(b_rest[:, i, :], b_bc, b_part[:, i, 0, :], ALU.subtract))
                then(nc.vector.tensor_copy(b_part[:, i, 1, :], b_rest[:, i, :]))
                then(nc.vector.tensor_tensor(b_part[:, i, 2, :], b_rest[:, i, :], b_part[:, i, 1, :], ALU.subtract))
                for part in range(3):
                    r = 32 * part
                    ins = nc.vector.tensor_copy(rows[r:r + 1, :, :],
                                                b_part[r:r + 1, i, part, :].unsqueeze(1).to_broadcast([1, 4, C]))
                ins.then_inc(b_split, 1)

            def table_rest(n):
                m = batch(n)
                dve.wait_ge(node_hi, n + 1)
                if n >= 2:
                    dve.wait_ge(node_lo, n - 1)
                nc.vector.tensor_tensor(tab_rest[:, n % 2, 0:m, :], wide_banks[(NQ + n) % 4][:, 0:m, :],
                                        tab_dst[:, n % NB, 0:m, 0, :], ALU.subtract).then_inc(node_r1, 1)

            def table_low(n):
                m = batch(n)
                dve.wait_ge(node_mid, n + 1)
                nc.vector.tensor_tensor(tab_dst[:, n % NB, 0:m, 2, :], tab_rest[:, n % 2, 0:m, :],
                                        tab_dst[:, n % NB, 0:m, 1, :], ALU.subtract).then_inc(node_lo, 1)

            def least_targets():
                dve.wait_ge(dsts_in, 16 * dst_pieces)
                nc.vector.tensor_reduce(dst_max[:], dst_s[:], AX.X, ALU.max)
                then(nc.vector.tensor_reduce(dst_min[:], dst_s[:], AX.X, ALU.min))
                then(nc.vector.tensor_reduce(base_col[:], dst_min[:], AX.X, ALU.min))
                dve.wait_ge(const_ok, 1)
                dve.wait_ge(ident_ok, 2)
                nc.vector.tensor_scalar(base_diag[:, 0:S], ident[0:S, 0:S], base_col[:, 0:1], None, ALU.mult)
                for i, lim in enumerate((dst_min, dst_max)):
                    ins = nc.vector.scalar_tensor_tensor(miss[:, i, :], lim[:], base_col[:, 0:1], win_off[0:S, :],
                                                         op0=ALU.subtract, op1=ALU.subtract)
                then(ins)
                nc.vector.tensor_scalar(miss[:, 0, :], miss[:, 0, :], 0.0, None, ALU.is_lt)
                then(nc.vector.tensor_scalar(miss[:, 1, :], miss[:, 1, :], float(W - 1), None, ALU.is_gt))
                nc.vector.tensor_reduce(base_diag[:, S:S + 1], miss[:].rearrange("s i k -> s (i k)"), AX.X,
                                        ALU.add).then_inc(base_set, 1)

            def windows():
                dve.wait_ge(turn_out, 4)
                then(nc.vector.tensor_tensor(dst_rel[:].rearrange("p s k t -> p s (k t)"),
                                             dst_f[:].rearrange("p (s m) -> p s m", s=S),
                                             base_bc[:].unsqueeze(2).to_broadcast([P, S, J * T]), ALU.subtract))
                for k in range(J):
                    off = float(HOP * k - MARGIN)
                    nc.vector.tensor_scalar(dst_rel[:, :, k, :], dst_rel[:, :, k, :], off, None, ALU.subtract)
                    ins = nc.vector.tensor_scalar(win_node[:, :, k], base_bc[0:W], iota_col[:, 0:1], off, ALU.add,
                                                  ALU.add)
                ins.then_inc(rel_ok, 1)

            centre((W1S, W1D), w1_in, 16)
            for n in range(NQ):
                if n not in ACT_BATCHES:
                    m = batch(n)
                    dve.wait_ge(node_A, n + 1)
                    if n >= NB:
                        dve.wait_ge(src_out[n % NB], 16 * (n // NB))
                    nc.vector.tensor_copy(tab_src[:, n % NB, 0:m, :],
                                          wide_banks[n % 4][:, 0:m, :]).then_inc(node_Ac[n % 4], 1)
                if n == 1:
                    centre((W2, B1, B2), w_in, 48)
                    dve.wait_ge(centred, 2)
                if n == 2:
                    dve.wait_ge(const_ok, 1)
                    split_bias(0, mid[:, B1, :], b1_rows)
                if n == 4:
                    least_targets()
                if n == 6:
                    split_bias(1, mid[:, B2, :], b2_rows)
                if n == 8:
                    nc.vector.tensor_copy(ident_bf[:], ident[:])
                    nc.vector.tensor_scalar(less_mean[:], ident[:], 1.0 / C, None, ALU.subtract)
            dve.wait_ge(base_ps, 1)
            nc.vector.tensor_copy(base_bc[:], ps_o[:, 0:S])
            nc.vector.tensor_copy(base_i[:], ps_o[0:1, 0:S + 1]).then_inc(base_ok, 1)
            dve.wait_ge(base_ok, 1)
            for n in range(NQ):
                table_rest(n)
                if n >= 1:
                    table_low(n - 1)
                if n == 5:
                    windows()
            table_low(NQ - 1)
            dve.wait_ge(v_in, 16 * 7)
            dve.wait_ge(rel_ok, 1)
            nc.vector.nop().then_inc(acc_done, 1)

            def step(r, counts, turns):
                for k in range(K):
                    g2_, g3, g5 = (Back(counts, turns, k, lag) for lag in (2, 3, 5))
                    b = k % 2
                    norm1, norm2 = live(r, k, 2), live(r, k, 5)
                    if norm1 or norm2:
                        cols = slice(0 if norm1 else 1, 2 if norm2 else 1)
                        dve.wait_ge(std_ready[g2_.place], g2_.count)
                        nc.vector.reciprocal(rstd[:, b, cols, :], std[:, b, cols, :]).then_inc(rstd_ready[g2_.place], 1)
                    if k % J == 2 and live(r, k, 7):
                        g7 = Back(counts, turns, k, 7)
                        dve.wait_ge(o_ready, g7.count)
                        part = acc[:, bass.ds(base, SPAN)]
                        nc.vector.tensor_tensor(part, part, ps_o[:, 0:SPAN], ALU.add).then_inc(acc_done, 1)
                    if live(r, k, 0):
                        dve.wait_ge(dstbc_in[k // 2], turns[0] * 16)
                        nc.vector.tensor_scalar(pick[:, k % 2, :], dst_bc[:, k, :],
                                                win_node[:].rearrange("p s k -> p (s k)")[:, bass.ds(r * K + k, 1)],
                                                None, ALU.is_equal).then_inc(pick_ready[k % J], 1)
                    if norm2:
                        tiles = bass.ds(r * (K * T) + (k - 5) * T, T)
                        onehot = seg[:, g5.place, :, :]
                        rel = dst_rel[:].rearrange("p s k t -> p (s k t)")[:, tiles]
                        nc.vector.tensor_tensor(onehot, iota_row[:].unsqueeze(1).to_broadcast([P, T, W]),
                                                rel.unsqueeze(2).to_broadcast([P, T, W]),
                                                ALU.is_equal).then_inc(onehot_ready[g5.place], 1)
                        dve.wait_ge(rstd_ready[g2_.place], g2_.count)
                        dve_scale2(ps_h[g5.buf], rstd[:, b, 1, :]).then_inc(t2_ready[g5.place], 1)
                    if live(r, k, 3):
                        dve.wait_ge(aff_ready[g3.place], g3.count)
                        dve_leaky1(g3.buf).then_inc(z_ready[g3.place], 1)
                    if norm2:
                        dve.wait_ge(t2_ready[g5.place], g5.count)
                        dve_shift2().then_inc(u2_ready[g5.place], 1)
                    if k % J == 1 and live(r, k, 6):
                        base = dve.value_load(base_i[0:1, bass.ds(r * (K // J) + (k - 6) // J, 1)], min_val=0,
                                              max_val=N - 1)
                    if norm2:
                        dve.wait_ge(onehot_ready[g5.place], g5.count)
                        nc.vector.tensor_tensor(onehot, onehot,
                                                ew_all[:, tiles].unsqueeze(2).to_broadcast([P, T, W]), ALU.mult)
                        dve.wait_ge(u2_ready[g5.place], g5.count)
                        dve_leaky2(g5.place).then_inc(y_ready[g5.place], 1)

            def fast():
                rounds(dve, step)
                dve.wait_ge(acc_done, S + 1)
                nc.vector.nop().then_inc(sums_done, 1)

            def general():
                nc.vector.tensor_scalar(dst_idx[:, 0:NT], dst_f[:], float(MARGIN), None, ALU.add).then_inc(dst_rows, 1)
                with dve.Fori(0, G) as g:
                    n = dve.snap(g + 1)
                    dve.wait_ge(gen["std1"], n)
                    nc.vector.reciprocal(rstd[:, 0, 0, :], std[:, 0, 0, :]).then_inc(gen["rstd1"], 1)
                    dve.wait_ge(gen["aff"], n)
                    dve_leaky1(0).then_inc(gen["z"], 1)
                    dve.wait_ge(gen["std2"], n)
                    nc.vector.reciprocal(rstd[:, 0, 1, :], std[:, 0, 1, :]).then_inc(gen["rstd2"], 1)
                    dve.wait_ge(gen["rstd2"], n)
                    dve_scale2(ps_h[0], rstd[:, 0, 1, :]).then_inc(gen["t2"], 1)
                    dve.wait_ge(gen["t2"], n)
                    dve_shift2().then_inc(gen["u2"], 1)
                    dve.wait_ge(gen["u2"], n)
                    dve_leaky2(0).then_inc(gen["y"], 1)
                    dve.wait_ge(gen["y"], n)
                    for t in range(T):
                        weighted = y[:, 0, t, :]
                        nc.vector.tensor_scalar(weighted, weighted, ew_all[:, bass.ds(g * T + t, 1)], None, ALU.mult)
                    with dve.Fori(0, NW) as w:
                        m = dve.snap(g * NW + w + 1)
                        for t in range(T):
                            ins = nc.vector.tensor_scalar(seg_wide[:, t, :], iota_wide[:], wide_off[:, bass.ds(w, 1)],
                                                          dst_f[:, bass.ds(g * T + t, 1)], ALU.add, ALU.is_equal)
                        ins.then_inc(gen["seg"], 1)
                        dve.wait_ge(gen["o"], m)
                        part = acc[:, bass.ds(w * WIDE + MARGIN, WIDE)]
                        nc.vector.tensor_tensor(part, part, ps_o[:], ALU.add).then_inc(gen["acc"], 1)
                        dve.wait_ge(gen["acc"], dve.snap(m + 1))
                nc.vector.nop().then_inc(sums_done, 1)

            both_paths(dve, fast, general)

            for n in range(NQ + 1):
                o = n - 1
                qo = o % 2
                if n < NQ:
                    m = batch(n)
                    q = n % 2
                    dve.wait_ge(fT_ready, n + 1)
                    for j in range(m):
                        ins = nc.vector.bn_stats(stf[:, q, j, :], wide_banks[n % 4][:, j, :])
                    ins.then_inc(stf_ready, 1)
                if n >= 1:
                    mo = batch(o)
                    dve.wait_ge(stdf_ready, n)
                    if o >= 2:
                        dve.wait_ge(fin_ready, o - 1)
                    nc.vector.reciprocal(rstdf[:, qo, 0:mo], stdf[:, qo, 0:mo]).then_inc(rstdf_ready, 1)
                if n < NQ:
                    dve.wait_ge(stf_ready, n + 1)
                    for j in range(m):
                        ins = nc.vector.bn_aggr(mvf[:, q, j, :], stf[:, q, j, :])
                    ins.then_inc(mvf_ready, 1)


_INS = ["x", "src", "dst", "edge_weight", "L0_gnn_w1", "L0_gnn_b1", "L0_gnn_g1", "L0_gnn_be1",
        "L0_gnn_w2", "L0_gnn_b2", "L0_gnn_g2", "L0_gnn_be2"]


def kernel(**inputs):
    import numpy as _np
    import concourse.bacc as _bacc
    from concourse.bass_utils import run_bass_kernel_spmd as _run

    nc = _bacc.Bacc("TRN2", target_bir_lowering=False, num_devices=1)
    arrays, args = {}, []
    for name in _INS:
        a = _np.ascontiguousarray(inputs[name])
        arrays[f"in_{name}"] = a
        args.append(nc.dram_tensor(f"in_{name}", a.shape, mybir.dt.from_np(a.dtype), kind="ExternalInput").ap())
    shape = inputs["x"].shape
    args.append(nc.dram_tensor("out_0", shape, F32, kind="ExternalOutput").ap())
    gnn_layer(nc, *args)
    r = _run(nc, [arrays], core_ids=[0])
    return r.results[0]["out_0"]
```
